# Optimizing a Trainium2 kernel written in Bass

```python
import numpy as np
import jax
import jax.numpy as jnp

def _softmax(x, axis=-1):
    return jax.nn.softmax(x, axis=axis)

def _gelu(x):
    return jax.nn.gelu(x, approximate=True)

def _silu(x):
    return jax.nn.silu(x)

def _sigmoid(x):
    return jax.nn.sigmoid(x)

def _layernorm(x, axis=-1, eps=1e-05):
    m = jnp.mean(x, axis=axis, keepdims=True)
    v = jnp.var(x, axis=axis, keepdims=True)
    return (x - m) / jnp.sqrt(v + eps)

def _scatter_add(tgt, idx, src, axis=0):
    return tgt.at[idx].add(src)

def _segment_sum(src, seg, n):
    return jax.ops.segment_sum(src, seg, n)
kernel_name = 'mk_dlrm_tower_d1_rec_r8_42e1bf'

def setup_inputs(seed: int=0):
    np.random.seed(seed)
    _w = jnp.asarray

    def _rec_inputs():
        import jax
        import jax.numpy as jnp
        _tk = jax.random.key(seed)
        ids = jnp.stack([jax.random.randint(jax.random.fold_in(_tk, 200 + f), (2048,), 0, v, jnp.int32) for f, v in enumerate([1250, 12500, 1000, 1250, 12500, 1000, 1000, 125000, 125000, 12500, 1250, 125000, 1250, 12500, 1000, 1000, 1250, 12500, 12500, 1000, 1250, 1250, 1000, 1250, 1000, 1250])], axis=1)
        tbl_0 = 0.05 * jax.random.normal(jax.random.fold_in(_tk, 500 + 0), (1250, 64), jnp.float32)
        tbl_1 = 0.05 * jax.random.normal(jax.random.fold_in(_tk, 500 + 1), (12500, 64), jnp.float32)
        tbl_2 = 0.05 * jax.random.normal(jax.random.fold_in(_tk, 500 + 2), (1000, 64), jnp.float32)
        tbl_3 = 0.05 * jax.random.normal(jax.random.fold_in(_tk, 500 + 3), (1250, 64), jnp.float32)
        tbl_4 = 0.05 * jax.random.normal(jax.random.fold_in(_tk, 500 + 4), (12500, 64), jnp.float32)
        tbl_5 = 0.05 * jax.random.normal(jax.random.fold_in(_tk, 500 + 5), (1000, 64), jnp.float32)
        tbl_6 = 0.05 * jax.random.normal(jax.random.fold_in(_tk, 500 + 6), (1000, 64), jnp.float32)
        tbl_7 = 0.05 * jax.random.normal(jax.random.fold_in(_tk, 500 + 7), (125000, 64), jnp.float32)
        tbl_8 = 0.05 * jax.random.normal(jax.random.fold_in(_tk, 500 + 8), (125000, 64), jnp.float32)
        tbl_9 = 0.05 * jax.random.normal(jax.random.fold_in(_tk, 500 + 9), (12500, 64), jnp.float32)
        tbl_10 = 0.05 * jax.random.normal(jax.random.fold_in(_tk, 500 + 10), (1250, 64), jnp.float32)
        tbl_11 = 0.05 * jax.random.normal(jax.random.fold_in(_tk, 500 + 11), (125000, 64), jnp.float32)
        tbl_12 = 0.05 * jax.random.normal(jax.random.fold_in(_tk, 500 + 12), (1250, 64), jnp.float32)
        tbl_13 = 0.05 * jax.random.normal(jax.random.fold_in(_tk, 500 + 13), (12500, 64), jnp.float32)
        tbl_14 = 0.05 * jax.random.normal(jax.random.fold_in(_tk, 500 + 14), (1000, 64), jnp.float32)
        tbl_15 = 0.05 * jax.random.normal(jax.random.fold_in(_tk, 500 + 15), (1000, 64), jnp.float32)
        tbl_16 = 0.05 * jax.random.normal(jax.random.fold_in(_tk, 500 + 16), (1250, 64), jnp.float32)
        tbl_17 = 0.05 * jax.random.normal(jax.random.fold_in(_tk, 500 + 17), (12500, 64), jnp.float32)
        tbl_18 = 0.05 * jax.random.normal(jax.random.fold_in(_tk, 500 + 18), (12500, 64), jnp.float32)
        tbl_19 = 0.05 * jax.random.normal(jax.random.fold_in(_tk, 500 + 19), (1000, 64), jnp.float32)
        tbl_20 = 0.05 * jax.random.normal(jax.random.fold_in(_tk, 500 + 20), (1250, 64), jnp.float32)
        tbl_21 = 0.05 * jax.random.normal(jax.random.fold_in(_tk, 500 + 21), (1250, 64), jnp.float32)
        tbl_22 = 0.05 * jax.random.normal(jax.random.fold_in(_tk, 500 + 22), (1000, 64), jnp.float32)
        tbl_23 = 0.05 * jax.random.normal(jax.random.fold_in(_tk, 500 + 23), (1250, 64), jnp.float32)
        tbl_24 = 0.05 * jax.random.normal(jax.random.fold_in(_tk, 500 + 24), (1000, 64), jnp.float32)
        tbl_25 = 0.05 * jax.random.normal(jax.random.fold_in(_tk, 500 + 25), (1250, 64), jnp.float32)
        _rk = jax.random.fold_in(_tk, 7)
        r_dense_t = 7.22013e-05 + 1.00017 * jax.random.normal(jax.random.fold_in(_rk, 101), (2048, 256), jnp.float32)
        W_top1 = 0.0360844 * jax.random.normal(jax.random.fold_in(_tk, 801), (768, 512), jnp.float32)
        W_top2 = 0.0441942 * jax.random.normal(jax.random.fold_in(_tk, 802), (512, 256), jnp.float32)
        W_top3 = 0.0625 * jax.random.normal(jax.random.fold_in(_tk, 803), (256, 1), jnp.float32)
        b_top1 = jnp.zeros((512,), jnp.float32)
        b_top2 = jnp.zeros((256,), jnp.float32)
        return (r_dense_t, ids, tbl_0, tbl_1, tbl_2, tbl_3, tbl_4, tbl_5, tbl_6, tbl_7, tbl_8, tbl_9, tbl_10, tbl_11, tbl_12, tbl_13, tbl_14, tbl_15, tbl_16, tbl_17, tbl_18, tbl_19, tbl_20, tbl_21, tbl_22, tbl_23, tbl_24, tbl_25, W_top1, b_top1, W_top2, b_top2, W_top3)
    r_dense_t, ids, tbl_0, tbl_1, tbl_2, tbl_3, tbl_4, tbl_5, tbl_6, tbl_7, tbl_8, tbl_9, tbl_10, tbl_11, tbl_12, tbl_13, tbl_14, tbl_15, tbl_16, tbl_17, tbl_18, tbl_19, tbl_20, tbl_21, tbl_22, tbl_23, tbl_24, tbl_25, W_top1, b_top1, W_top2, b_top2, W_top3 = _rec_inputs()

    def _L0_rec_setup():
        import jax, jax.numpy as jnp
        import numpy as np
        EPS = 1e-05
        NI = 33
        TRIL_I, TRIL_J = np.tril_indices(NI, k=-1)

        def layer_norm(x, g, b):
            m = jnp.mean(x, axis=-1, keepdims=True)
            v = jnp.mean(jnp.square(x - m), axis=-1, keepdims=True)
            return (x - m) * jax.lax.rsqrt(v + EPS) * g + b
        key = jax.random.key(seed)
        ks = jax.random.split(key, 8)
        B, D_DENSE, N_SP, D_SP = (4096, 256, 26, 64)
        E, PROJ, MAXD, NFLAT = (128, 32, 512, 528)
        dense_t = jax.random.normal(ks[0], (B, D_DENSE), dtype=jnp.float32)
        sparse_t = jax.random.normal(ks[1], (B, N_SP, D_SP), dtype=jnp.float32)
        Wd = jax.random.normal(ks[2], (E, D_DENSE), dtype=jnp.float32) / np.sqrt(D_DENSE)
        Ws = jax.random.normal(ks[3], (E, D_SP), dtype=jnp.float32) / np.sqrt(D_SP)
        Wsi = jax.random.normal(ks[4], (PROJ, N_SP), dtype=jnp.float32) / np.sqrt(N_SP)
        Wl = jax.random.normal(ks[5], (MAXD, NFLAT), dtype=jnp.float32) / np.sqrt(NFLAT)
        gd = jnp.ones((E,), jnp.float32)
        bd = jnp.zeros((E,), jnp.float32)
        gs = jnp.ones((E,), jnp.float32)
        bs = jnp.zeros((E,), jnp.float32)
        gsi = jnp.ones((PROJ,), jnp.float32)
        bsi = jnp.zeros((PROJ,), jnp.float32)
        gl = jnp.ones((MAXD,), jnp.float32)
        bl = jnp.zeros((MAXD,), jnp.float32)
        return {'dense_t': dense_t, 'sparse_t': sparse_t, 'Wd': Wd, 'gd': gd, 'bd': bd, 'Ws': Ws, 'gs': gs, 'bs': bs, 'Wsi': Wsi, 'gsi': gsi, 'bsi': bsi, 'Wl': Wl, 'gl': gl, 'bl': bl, 'dims_in_use': 384}
    _L0_rec_all = _L0_rec_setup()
    _L0_rec_in = {k: v for k, v in _L0_rec_all.items() if k in ('Wd', 'gd', 'bd', 'Ws', 'gs', 'bs', 'Wsi', 'gsi', 'bsi', 'Wl', 'gl', 'bl')}
    del _L0_rec_all
    return {'r_dense_t': r_dense_t, 'ids': ids, 'tbl_0': tbl_0, 'tbl_1': tbl_1, 'tbl_2': tbl_2, 'tbl_3': tbl_3, 'tbl_4': tbl_4, 'tbl_5': tbl_5, 'tbl_6': tbl_6, 'tbl_7': tbl_7, 'tbl_8': tbl_8, 'tbl_9': tbl_9, 'tbl_10': tbl_10, 'tbl_11': tbl_11, 'tbl_12': tbl_12, 'tbl_13': tbl_13, 'tbl_14': tbl_14, 'tbl_15': tbl_15, 'tbl_16': tbl_16, 'tbl_17': tbl_17, 'tbl_18': tbl_18, 'tbl_19': tbl_19, 'tbl_20': tbl_20, 'tbl_21': tbl_21, 'tbl_22': tbl_22, 'tbl_23': tbl_23, 'tbl_24': tbl_24, 'tbl_25': tbl_25, 'W_top1': W_top1, 'b_top1': b_top1, 'W_top2': W_top2, 'b_top2': b_top2, 'W_top3': W_top3, 'L0_rec_Wd': _L0_rec_in['Wd'], 'L0_rec_gd': _L0_rec_in['gd'], 'L0_rec_bd': _L0_rec_in['bd'], 'L0_rec_Ws': _L0_rec_in['Ws'], 'L0_rec_gs': _L0_rec_in['gs'], 'L0_rec_bs': _L0_rec_in['bs'], 'L0_rec_Wsi': _L0_rec_in['Wsi'], 'L0_rec_gsi': _L0_rec_in['gsi'], 'L0_rec_bsi': _L0_rec_in['bsi'], 'L0_rec_Wl': _L0_rec_in['Wl'], 'L0_rec_gl': _L0_rec_in['gl'], 'L0_rec_bl': _L0_rec_in['bl']}

def reference(r_dense_t, ids, tbl_0, tbl_1, tbl_2, tbl_3, tbl_4, tbl_5, tbl_6, tbl_7, tbl_8, tbl_9, tbl_10, tbl_11, tbl_12, tbl_13, tbl_14, tbl_15, tbl_16, tbl_17, tbl_18, tbl_19, tbl_20, tbl_21, tbl_22, tbl_23, tbl_24, tbl_25, W_top1, b_top1, W_top2, b_top2, W_top3, L0_rec_Wd, L0_rec_gd, L0_rec_bd, L0_rec_Ws, L0_rec_gs, L0_rec_bs, L0_rec_Wsi, L0_rec_gsi, L0_rec_bsi, L0_rec_Wl, L0_rec_gl, L0_rec_bl):
    import jax
    import jax.numpy as jnp

    def _L0_rec_ref(dense_t, sparse_t, Wd, gd, bd, Ws, gs, bs, Wsi, gsi, bsi, Wl, gl, bl, dims_in_use):
        import jax, jax.numpy as jnp
        import numpy as np
        EPS = 1e-05
        NI = 33
        TRIL_I, TRIL_J = np.tril_indices(NI, k=-1)

        def layer_norm(x, g, b):
            m = jnp.mean(x, axis=-1, keepdims=True)
            v = jnp.mean(jnp.square(x - m), axis=-1, keepdims=True)
            return (x - m) * jax.lax.rsqrt(v + EPS) * g + b
        x = layer_norm(dense_t @ Wd.T, gd, bd)
        y = layer_norm(jnp.einsum('bnd,ed->bne', sparse_t, Ws), gs, bs)
        y = jnp.einsum('bne,pn->bep', y, Wsi)
        y = layer_norm(y, gsi, bsi)
        y = jnp.swapaxes(y, 1, 2)
        T = jnp.concatenate([x[:, None, :], y], axis=1)
        Z = jnp.einsum('bnd,bmd->bnm', T, T)
        Zflat = Z[:, TRIL_I, TRIL_J]
        out = layer_norm(Zflat @ Wl.T, gl, bl)
        maxd = out.shape[-1]
        mask = (jnp.arange(maxd) < dims_in_use).astype(out.dtype)
        return out * mask
    e = jnp.stack([tbl_0[ids[:, 0]], tbl_1[ids[:, 1]], tbl_2[ids[:, 2]], tbl_3[ids[:, 3]], tbl_4[ids[:, 4]], tbl_5[ids[:, 5]], tbl_6[ids[:, 6]], tbl_7[ids[:, 7]], tbl_8[ids[:, 8]], tbl_9[ids[:, 9]], tbl_10[ids[:, 10]], tbl_11[ids[:, 11]], tbl_12[ids[:, 12]], tbl_13[ids[:, 13]], tbl_14[ids[:, 14]], tbl_15[ids[:, 15]], tbl_16[ids[:, 16]], tbl_17[ids[:, 17]], tbl_18[ids[:, 18]], tbl_19[ids[:, 19]], tbl_20[ids[:, 20]], tbl_21[ids[:, 21]], tbl_22[ids[:, 22]], tbl_23[ids[:, 23]], tbl_24[ids[:, 24]], tbl_25[ids[:, 25]]], axis=1)
    z = _L0_rec_ref(r_dense_t, e, L0_rec_Wd, L0_rec_gd, L0_rec_bd, L0_rec_Ws, L0_rec_gs, L0_rec_bs, L0_rec_Wsi, L0_rec_gsi, L0_rec_bsi, L0_rec_Wl, L0_rec_gl, L0_rec_bl, 384)
    z = z.reshape(z.shape[0], -1)
    h = jnp.concatenate([z, r_dense_t], axis=1)
    h = jnp.maximum(h @ W_top1 + b_top1, 0.0)
    h = jnp.maximum(h @ W_top2 + b_top2, 0.0)
    y = h @ W_top3
    return y

_drawn_inputs = setup_inputs


def setup_inputs(seed=0):
    import zlib

    import numpy as np

    out = dict(_drawn_inputs(seed))
    spreads = {'b_top1': (0.0, 0.1),
     'b_top2': (0.0, 0.1),
     'L0_rec_gd': (1.0, 0.6),
     'L0_rec_bd': (0.0, 0.8),
     'L0_rec_gs': (1.0, 0.6),
     'L0_rec_bs': (0.0, 0.1),
     'L0_rec_gsi': (1.0, 0.2),
     'L0_rec_bsi': (0.0, 0.1),
     'L0_rec_gl': (1.0, 0.2),
     'L0_rec_bl': (0.0, 0.1)}
    factors = {}
    for name, (base, spread) in spreads.items():
        noise = np.random.default_rng([zlib.crc32(name.encode()), seed]).standard_normal(out[name].shape)
        drawn = base * np.exp(spread * noise) if base else spread * noise
        out[name] = jnp.asarray(drawn.astype(out[name].dtype))
    for name, factor in factors.items():
        out[name] = (out[name] * factor).astype(out[name].dtype)
    return out
```

```python
import concourse.bass as bass
from concourse import mybir
from contextlib import ExitStack

F32 = mybir.dt.float32
I32 = mybir.dt.int32
ALU = mybir.AluOpType
ACT = mybir.ActivationFunctionType
AX = mybir.AxisListType

B, DENSE, NF, D, E, P = 2048, 256, 26, 64, 128, 32
MAXD, DIMS = 512, 384
H1, H2 = 512, 256
EPS = 1e-5
BLK = 128
NBLK = B // BLK
STEPS = 4
J = 4
ROWS = J * NF
GA = 8
SPS = J * GA
PAIRS = GA // 2
TC = P + 2
NS = NBLK * STEPS
KP = 5
KL = 2 * P + 2
ZK = DIMS // 128
DK = DENSE // 128
DMA = 16


def pair_tiles():
    tiles = [[(q, p) for q in range(0, 4) for p in range(32)],
             [(q, p) for q in range(4, 8) for p in range(32)],
             [(q, p) for q in range(8, 16) for p in range(8, 24)],
             [(q, p) for q in range(16, 24) for p in range(16, 32)],
             [(q, p) for q in list(range(8, 16)) + list(range(24, 32)) for p in range(24, 32)]]
    return tiles


def pair_slices(zt):
    full = zt[:, 0:P * P].rearrange("s (q p) -> s q p", p=P)
    halves = zt[:, 0:P * P].rearrange("s (a b p) -> s a b p", b=8, p=P)
    return [full[:, 8:16, 8:24], full[:, 16:24, 16:32], halves[:, 1:4:2, :, 24:32]]


def dlrm_kernel(nc, dense_t, ids, row_base, tables, ws_t, gs, bs, wsi_t, wd_t, gd, bd, wl_pairs,
                g_of_p, g_of_q, b_of_p, b_of_q, is_p, is_q, gsi, identity, gl, bl, w1, b1, w2, b2, w3, out):
    ctx = ExitStack()

    def sb(name, shape, dt=F32):
        return ctx.enter_context(nc.sbuf_tensor(name, shape, dt))

    def pb(name, shape):
        return ctx.enter_context(nc.psum_tensor(name, shape, F32))

    def sem(name):
        return ctx.enter_context(nc.semaphore(name))

    with ctx:
        ident = sb("ident", [128, 128])
        feature_id = sb("feature_id", [ROWS, NBLK * STEPS * GA], I32)
        rows = [sb(f"rows{k}", [ROWS, GA], I32) for k in range(STEPS)]
        base = sb("base", [ROWS, 1], I32)
        wc = sb("wc", [2 * D, E])
        wcg = sb("wcg", [2 * D, E])
        wc_e = sb("wc_e", [E, 2 * D])
        gram_w = sb("gram_w", [2 * D, 2 * D])
        half_ones = sb("half_ones", [2 * D, 2])
        proj = sb("proj", [ROWS, J, P])
        proj_mean = sb("proj_mean", [ROWS, J])
        gs_b = sb("gs_b", [2 * D, E])
        bs_b = sb("bs_b", [NF, E])
        y_bias = sb("y_bias", [E, P])
        wd = sb("wd", [128, DK, E])
        wd_mean = sb("wd_mean", [128, DK])
        wc_mean = sb("wc_mean", [2 * D, 1])
        gd_c = sb("gd_c", [E, 1])
        bd_c = sb("bd_c", [E, 1])
        mean_ones = sb("mean_ones", [E, E])
        ones = sb("ones", [E, 1])
        wl = sb("wl", [128, KP + 1, MAXD])
        gp = sb("gp", [128, KP + 1])
        gq = sb("gq", [128, KP + 1])
        bp = sb("bp", [128, KP + 1])
        bq = sb("bq", [128, KP + 1])
        isp = sb("isp", [128, KP + 1, P])
        isq = sb("isq", [128, KP + 1, P])
        coef = sb("coef", [128, 4, KP + 1])
        fold = sb("fold", [128, KP + 1, KL])
        fold_q = sb("fold_q", [128, KP, P])
        w1_s = sb("w1_s", [128, ZK + DK, H1])
        gl_c = sb("gl_c", [128, ZK])
        bl_c = sb("bl_c", [128, ZK])
        b1_c = sb("b1_c", [128, H1 // 128])
        b1_f = sb("b1_f", [128, H1 // 128])
        w2_s = sb("w2_s", [128, H1 // 128, H2])
        b2_c = sb("b2_c", [128, H2 // 128])
        w3_s = sb("w3_s", [128, H2 // 128])
        emb = [sb(f"emb{k}", [ROWS, GA, D]) for k in range(STEPS)]
        emb_t = [sb(f"emb_t{i}", [2 * D, PAIRS * ROWS]) for i in range(2)]
        quad = [sb(f"quad{i}", [2 * D, PAIRS * ROWS]) for i in range(2)]
        eps = sb("eps", [128, 1])
        std = sb("std", [ROWS, GA])
        rstd = sb("rstd", [ROWS, GA])
        emb_r = [sb(f"emb_r{i}", [ROWS, GA, D]) for i in range(2)]
        mix = [sb(f"mix{i}", [2 * D, PAIRS * J * P]) for i in range(2)]
        y = sb("y", [E, SPS, P])
        ysq = sb("ysq", [E, SPS, P])
        yvar = sb("yvar", [E, SPS])
        ystd = sb("ystd", [E, SPS])
        yrstd = sb("yrstd", [E, SPS])
        v = [sb(f"v{i}", [E, SPS, TC]) for i in range(2)]
        dense_x = sb("dense_x", [128, DK, BLK])
        dense_h = sb("dense_h", [128, DK, BLK])
        xsq = sb("xsq", [E, BLK])
        xstd = sb("xstd", [E, BLK])
        xrstd = sb("xrstd", [E, BLK])
        x_scaled = sb("x_scaled", [E, BLK])
        x = sb("x", [E, BLK])
        gram = sb("gram", [128, TC, BLK // J])
        zt = sb("zt", [BLK, TC * P + 2])
        zc = sb("zc", [BLK, 3, 128])
        zk = sb("zk", [128, KP + 1, BLK])
        stats = sb("stats", [BLK, 6])
        mv = sb("mv", [BLK, 2])
        zstd = sb("zstd", [BLK, 1])
        zrstd = sb("zrstd", [BLK, 1])
        zshift = sb("zshift", [BLK, 1])
        z = sb("z", [BLK, DIMS])
        z_t = sb("z_t", [128, ZK, BLK])
        h1 = sb("h1", [128, H1 // 128, BLK])
        h2 = sb("h2", [128, H2 // 128, BLK])
        score = sb("score", [1, BLK])
        ps_t = pb("ps_t", [128, 512])
        ps_q = pb("ps_q", [128, 512])
        ps_m = pb("ps_m", [128, 512])
        ps_y = pb("ps_y", [128, 1024])
        ps_z = pb("ps_z", [128, 512])
        ps_a = pb("ps_a", [128, 512])
        ps_b = pb("ps_b", [128, 512])
        var_at = PAIRS * ROWS
        ps_var = ps_q[0:ROWS, var_at:var_at + GA]
        ps_sum = ps_b[:, 0:1]
        ps_x = ps_b[:, 384:512]
        ps_xv = ps_b[:, 256:384]

        ids_in = sem("ids_in")
        interaction_w_in = sem("interaction_w_in")
        x_w_in = sem("x_w_in")
        wl_in = sem("wl_in")
        mlp_w_in = sem("mlp_w_in")
        dense_x_in = sem("dense_x_in")
        dense_h_in = sem("dense_h_in")
        gathered = [sem(f"gathered{k}") for k in range(STEPS)]
        out_done = sem("out_done")
        prep_dve = sem("prep_dve")
        prep_pe = sem("prep_pe")
        prep_act = sem("prep_act")
        rows_ready = sem("rows_ready")
        emb_t_psum = sem("emb_t_psum")
        emb_t_ready = sem("emb_t_ready")
        q_psum = sem("q_psum")
        quad_ready = sem("quad_ready")
        var_psum = sem("var_psum")
        std_ready = sem("std_ready")
        rstd_ready = sem("rstd_ready")
        emb_r_ready = sem("emb_r_ready")
        mix_psum = sem("mix_psum")
        mix_ready = sem("mix_ready")
        y_psum = sem("y_psum")
        y_ready = sem("y_ready")
        ysq_ready = sem("ysq_ready")
        yvar_ready = sem("yvar_ready")
        ystd_ready = sem("ystd_ready")
        yrstd_ready = sem("yrstd_ready")
        v_ready = sem("v_ready")
        gram_psum = sem("gram_psum")
        gram_ready = sem("gram_ready")
        x_psum = sem("x_psum")
        xsq_ready = sem("xsq_ready")
        xvar_psum = sem("xvar_psum")
        xstd_ready = sem("xstd_ready")
        xrstd_ready = sem("xrstd_ready")
        x_scaled_ready = sem("x_scaled_ready")
        x_ready = sem("x_ready")
        sumx_psum = sem("sumx_psum")
        sumx_ready = sem("sumx_ready")
        zt_ready = sem("zt_ready")
        zc_ready = sem("zc_ready")
        zk_psum = sem("zk_psum")
        zk_ready = sem("zk_ready")
        z_psum = sem("z_psum")
        stats_ready = sem("stats_ready")
        mv_ready = sem("mv_ready")
        zstd_ready = sem("zstd_ready")
        zrstd_ready = sem("zrstd_ready")
        zshift_ready = sem("zshift_ready")
        z_ready = sem("z_ready")
        z_t_psum = sem("z_t_psum")
        z_t_ready = sem("z_t_ready")
        h1_psum = sem("h1_psum")
        h1_ready = sem("h1_ready")
        h2_psum = sem("h2_psum")
        h2_ready = sem("h2_ready")
        score_psum = sem("score_psum")
        score_ready = sem("score_ready")

        DVE_CONST, DVE_WC, DVE_GRAM, DVE_PROJ, DVE_WD, DVE_YBIAS, DVE_FOLD, DVE_WL, DVE_W1 = 1, 4, 6, 9, 11, 12, 17, 19, 20
        PE_WCE, PE_GRAM, PE_YBIAS, PE_FOLD, PE_B1 = 1, 2, 3, 4, 5
        ACT_WCE, ACT_FOLD = 1, 2

        def wait(engine, semaphore, count):
            if not isinstance(count, int) or count > 0:
                engine.wait_ge(semaphore, count)

        def blocks(engine, body):
            body(0, True, False)
            body(1, False, False)
            with engine.Fori(2, NBLK - 1) as b:
                body(b, False, False)
            body(NBLK - 1, False, True)

        block = ctx.enter_context(nc.Block())

        @block.sync
        def _(sp):
            sp.dma_start(feature_id[:, :], ids).then_inc(ids_in, DMA)
            sp.dma_start(base[:, :], row_base).then_inc(ids_in, DMA)
            sp.dma_start(dense_x[:, :, :], dense_t[:, :, 0:BLK]).then_inc(dense_x_in, DMA)
            sp.dma_start(wd[:, :, :], wd_t).then_inc(x_w_in, DMA)
            sp.dma_start(gd_c[:, :], gd).then_inc(x_w_in, DMA)
            sp.dma_start(bd_c[:, :], bd).then_inc(x_w_in, DMA)
            sp.dma_start(w1_s[:, :, :], w1).then_inc(mlp_w_in, DMA)
            sp.dma_start(w2_s[:, :, :], w2).then_inc(mlp_w_in, DMA)
            sp.dma_start(w3_s[:, :], w3).then_inc(mlp_w_in, DMA)
            sp.dma_start(gl_c[:, :], gl).then_inc(mlp_w_in, DMA)
            sp.dma_start(bl_c[:, :], bl).then_inc(mlp_w_in, DMA)
            sp.dma_start(b1_c[:, :], b1).then_inc(mlp_w_in, DMA)
            sp.dma_start(b2_c[:, :], b2).then_inc(mlp_w_in, DMA)

            def dense_for_x(b):
                sp.wait_ge(x_psum, b)
                sp.dma_start(dense_x[:, :, :], dense_t[:, :, bass.ds(b * BLK, BLK)]).then_inc(dense_x_in, DMA)

            def body(b, first, last):
                if first:
                    dense_for_x(1)
                if not last:
                    dense_for_x(b + 2)
                wait(sp, h1_psum, b)
                sp.dma_start(dense_h[:, :, :], dense_t[:, :, bass.ds(b * BLK, BLK)]).then_inc(dense_h_in, DMA)
                if not first:
                    sp.wait_ge(score_ready, b)
                    sp.dma_start(out[:, bass.ds((b - 1) * BLK, BLK)], score[:, :]).then_inc(out_done, DMA)

            body(0, True, False)
            with sp.Fori(1, NBLK - 2) as b:
                body(b, False, False)
            body(NBLK - 2, False, True)
            body(NBLK - 1, False, True)
            sp.wait_ge(score_ready, NBLK)
            sp.dma_start(out[:, (NBLK - 1) * BLK:B], score[:, :]).then_inc(out_done, DMA)
            sp.wait_ge(out_done, DMA * NBLK)

        @block.gpsimd
        def _(pool):
            pool.wait_ge(ids_in, 2 * DMA)

            def body(b, first, last):
                for k in range(STEPS):
                    if not first:
                        pool.wait_ge(gathered[k], GA * DMA * b)
                    pool.tensor_tensor(rows[k][:, :], feature_id[:, bass.ds(b * (STEPS * GA) + k * GA, GA)],
                                       base[:, 0:1].to_broadcast([ROWS, GA]), ALU.add).then_inc(rows_ready, 1)
                    if not first:
                        pool.wait_ge(emb_r_ready, 4 * b - 3 + k)
                    pool.wait_ge(rows_ready, 4 * b + k + 1)
                    pool.nop(nofuse=True)
                    for g in range(GA):
                        pool.indirect_dma_start(
                            out=emb[k][:, g, :], out_offset=None, in_=tables,
                            in_offset=bass.IndirectOffsetOnAxis(ap=rows[k][:, g:g + 1], axis=0),
                        ).then_inc(gathered[k], DMA)

            blocks(pool, body)

        @block.scalar
        def _(act):
            act.dma_start(wc[0:D, :], ws_t).then_inc(interaction_w_in, DMA)
            act.dma_start(wc[D:2 * D, :], ws_t).then_inc(interaction_w_in, DMA)
            act.dma_start(ident[:, :], identity).then_inc(interaction_w_in, DMA)
            act.dma_start(gs_b[:, :], gs.partition_broadcast(2 * D)).then_inc(interaction_w_in, DMA)
            act.dma_start(bs_b[:, :], bs.partition_broadcast(NF)).then_inc(interaction_w_in, DMA)
            act.wait_ge(prep_dve, DVE_CONST)
            for j in range(J):
                act.dma_start(proj[j * NF:(j + 1) * NF, j, :], wsi_t).then_inc(interaction_w_in, DMA)
            act.dma_start(wl[:, :, :], wl_pairs).then_inc(wl_in, DMA)
            for tile, source in ((gp, g_of_p), (gq, g_of_q), (bp, b_of_p), (bq, b_of_q)):
                act.dma_start(tile[:, :], source).then_inc(wl_in, DMA)
            act.dma_start(isp[:, :, :], is_p).then_inc(wl_in, DMA)
            act.dma_start(isq[:, :, :], is_q).then_inc(wl_in, DMA)

            def copy_emb_t(s, par):
                act.wait_ge(emb_t_psum, s + 1)
                wait(act, quad_ready, s - 1)
                nc.scalar.copy(emb_t[par][:, :], ps_t[:, 0:PAIRS * ROWS]).then_inc(emb_t_ready, 1)

            def copy_mix(s, par):
                act.wait_ge(mix_psum, s + 1)
                wait(act, y_psum, 2 * s - 2)
                nc.scalar.copy(mix[par][:, :], ps_m[:, :]).then_inc(mix_ready, 1)

            def std_emb(s):
                act.wait_ge(var_psum, s + 1)
                wait(act, rstd_ready, s)
                nc.scalar.activation(std[:, :], ps_var, ACT.Sqrt, bias=eps[0:ROWS, 0:1]).then_inc(std_ready, 1)

            def std_y(s):
                act.wait_ge(yvar_ready, s + 1)
                wait(act, yrstd_ready, s)
                nc.scalar.activation(ystd[:, :], yvar[:, :], ACT.Sqrt, bias=eps[:, 0:1],
                                     scale=1.0 / P).then_inc(ystd_ready, 1)

            def std_x(b):
                act.wait_ge(xvar_psum, b + 1)
                wait(act, xrstd_ready, b)
                nc.scalar.activation(xstd[:, :], ps_xv, ACT.Sqrt, bias=eps[:, 0:1]).then_inc(xstd_ready, 1)

            def std_z(b):
                act.wait_ge(mv_ready, b + 1)
                wait(act, zrstd_ready, b)
                nc.scalar.activation(zstd[:, :], mv[:, 1:2], ACT.Sqrt, bias=eps[:, 0:1]).then_inc(zstd_ready, 1)

            def square_y(s, h):
                act.wait_ge(y_ready, 2 * s + 1 + h)
                if h == 0:
                    wait(act, yvar_ready, s)
                c = slice(h * SPS // 2, (h + 1) * SPS // 2)
                nc.scalar.activation(ysq[:, c, :], y[:, c, :], ACT.Square).then_inc(ysq_ready, 1)

            def copy_gram(s, b, k):
                act.wait_ge(gram_psum, s + 1)
                if k == 0:
                    wait(act, zt_ready, b)
                src = ps_z[:, 0:GA * TC].rearrange("p (g q) -> p q g", q=TC)
                nc.scalar.copy(gram[:, :, k * GA:(k + 1) * GA], src).then_inc(gram_ready, 1)

            def square_x(b):
                act.wait_ge(x_psum, b + 1)
                wait(act, xvar_psum, b)
                nc.scalar.activation(xsq[:, :], ps_x, ACT.Square).then_inc(xsq_ready, 1)

            def copy_zk(b):
                act.wait_ge(zk_psum, b + 1)
                wait(act, z_psum, b)
                nc.scalar.copy(zk[:, 0:4, :], ps_a[:, :].rearrange("p (t s) -> p t s", t=4))
                nc.scalar.copy(zk[:, 4, :], ps_b[:, 0:BLK])
                nc.scalar.copy(zk[0:KL, 5, :], ps_b[0:KL, BLK:2 * BLK]).then_inc(zk_ready, 1)

            def normalise_z(b):
                act.wait_ge(zshift_ready, b + 1)
                wait(act, z_t_psum, b)
                nc.scalar.activation(z[:, :], ps_a[:, 0:DIMS], ACT.Identity, bias=zshift[:, 0:1],
                                     scale=zrstd[:, 0:1]).then_inc(z_ready, 1)

            def copy_z_t(b):
                act.wait_ge(z_t_psum, b + 1)
                wait(act, h1_psum, b)
                nc.scalar.copy(z_t[:, :, :], ps_b[:, 0:DIMS].rearrange("p (t s) -> p t s", t=ZK)).then_inc(z_t_ready, 1)

            def relu_h1(b):
                act.wait_ge(h1_psum, b + 1)
                wait(act, h2_psum, b)
                for m in range(H1 // 128):
                    last = nc.scalar.activation(h1[:, m, :], ps_a[:, m * BLK:(m + 1) * BLK], ACT.Relu,
                                                bias=b1_f[:, m:m + 1])
                last.then_inc(h1_ready, 1)

            def relu_h2(b):
                act.wait_ge(h2_psum, b + 1)
                wait(act, score_psum, b)
                for m in range(H2 // 128):
                    last = nc.scalar.activation(h2[:, m, :], ps_a[:, m * BLK:(m + 1) * BLK], ACT.Relu,
                                                bias=b2_c[:, m:m + 1])
                last.then_inc(h2_ready, 1)

            def copy_score(b):
                act.wait_ge(score_psum, b + 1)
                wait(act, out_done, DMA * b)
                nc.scalar.copy(score[:, :], ps_a[0:1, 256:384]).then_inc(score_ready, 1)

            act.wait_ge(prep_pe, PE_WCE)
            nc.scalar.copy(wc_e[:, :], ps_a[:, 0:2 * D]).then_inc(prep_act, 1)
            square_x(0)
            copy_emb_t(0, 0)
            copy_emb_t(1, 1)
            std_emb(0)
            std_x(0)
            copy_mix(0, 0)
            copy_emb_t(2, 0)
            std_emb(1)
            act.wait_ge(mlp_w_in, 7 * DMA)

            def body(b, first, last):
                b2 = not isinstance(b, int) or b >= 2
                for k in range(STEPS):
                    i = 4 * b + k
                    if k == 0 and b2:
                        relu_h1(b - 2)
                    square_y(i, 0)
                    square_y(i, 1)
                    if not (last and k >= 2):
                        std_emb(i + 2)
                    if k == 0:
                        if b2:
                            relu_h2(b - 2)
                        if not last:
                            square_x(b + 1)
                    std_y(i)
                    if not (last and k >= 1):
                        copy_emb_t(i + 3, (k + 1) % 2)
                    if not (last and k == 3):
                        copy_mix(i + 1, (k + 1) % 2)
                    if k == 0:
                        if b2:
                            copy_score(b - 2)
                        if not last:
                            std_x(b + 1)
                    if k == 1 and not first:
                        copy_zk(b - 1)
                    if k == 2 and not first:
                        std_z(b - 1)
                    if k > 0:
                        copy_gram(i - 1, b, k - 1)
                    elif not first:
                        copy_gram(i - 1, b - 1, STEPS - 1)
                    if k == 2 and not first:
                        normalise_z(b - 1)
                        copy_z_t(b - 1)
                if first:
                    act.wait_ge(prep_pe, PE_FOLD)
                    nc.scalar.copy(wl[0:KL, KP, :], ps_a[0:KL, :]).then_inc(prep_act, 1)

            blocks(act, body)
            b = NBLK - 1
            relu_h1(b - 1)
            copy_gram(NS - 1, b, STEPS - 1)
            relu_h2(b - 1)
            copy_score(b - 1)
            copy_zk(b)
            std_z(b)
            normalise_z(b)
            copy_z_t(b)
            relu_h1(b)
            relu_h2(b)
            copy_score(b)

        @block.vector
        def _(dve):
            def quad_form(s, par):
                dve.wait_ge(q_psum, s + 1)
                wait(dve, var_psum, s - 1)
                nc.vector.tensor_tensor(quad[par][:, :], ps_q[:, 0:PAIRS * ROWS], emb_t[par][:, :],
                                        ALU.mult).then_inc(quad_ready, 1)

            def scale_emb(s, k, par):
                dve.wait_ge(std_ready, s + 1)
                nc.vector.reciprocal(rstd[:, :], std[:, :]).then_inc(rstd_ready, 1)
                wait(dve, mix_psum, s - 1)
                dve.wait_ge(rstd_ready, s + 1)
                nc.vector.tensor_tensor(emb_r[par][:, :, :], emb[k][:, :, :],
                                        rstd[:, :].unsqueeze(2).to_broadcast([ROWS, GA, D]),
                                        ALU.mult).then_inc(emb_r_ready, 1)

            def bias_y(s, h):
                if h == 0:
                    wait(dve, v_ready, s)
                dve.wait_ge(y_psum, 2 * s + 1 + h)
                n = SPS // 2
                src = ps_y[:, h * 512:(h + 1) * 512].rearrange("e (s p) -> e s p", p=P)
                nc.vector.tensor_tensor(y[:, h * n:(h + 1) * n, :], src,
                                        y_bias[:, :].unsqueeze(1).to_broadcast([E, n, P]),
                                        ALU.add).then_inc(y_ready, 1)

            def sum_squares(s):
                dve.wait_ge(ysq_ready, 2 * s + 2)
                nc.vector.tensor_reduce(yvar[:, :], ysq[:, :, :], AX.X, ALU.add).then_inc(yvar_ready, 1)

            def normalise_y(s, b, k, par):
                wait(dve, gram_psum, s - 1)
                dve.wait_ge(x_ready, b + 1)
                xk = x[:, :].rearrange("e (j k t h) -> e k h t j", j=J, k=STEPS, h=2)[:, k]
                nc.vector.tensor_copy(v[par][:, :, P].rearrange("e (h t j) -> e h t j", h=2, j=J), xk)
                dve.wait_ge(ystd_ready, s + 1)
                nc.vector.reciprocal(yrstd[:, :], ystd[:, :]).then_inc(yrstd_ready, 1)
                dve.wait_ge(yrstd_ready, s + 1)
                nc.vector.tensor_tensor(v[par][:, :, 0:P], y[:, :, :],
                                        yrstd[:, :].unsqueeze(2).to_broadcast([E, SPS, P]),
                                        ALU.mult).then_inc(v_ready, 1)

            def scale_x(b):
                dve.wait_ge(xstd_ready, b + 1)
                nc.vector.reciprocal(xrstd[:, :], xstd[:, :]).then_inc(xrstd_ready, 1)
                dve.wait_ge(xrstd_ready, b + 1)
                nc.vector.tensor_tensor(x_scaled[:, :], ps_x, xrstd[:, :], ALU.mult).then_inc(x_scaled_ready, 1)

            def finish_x(b):
                dve.wait_ge(x_scaled_ready, b + 1)
                wait(dve, sumx_psum, b)
                nc.vector.tensor_scalar(x[:, :], x_scaled[:, :], gd_c[:, 0:1], bd_c[:, 0:1],
                                        ALU.mult, ALU.add).then_inc(x_ready, 1)

            def copy_sumx(b):
                dve.wait_ge(sumx_psum, b + 1)
                wait(dve, zk_psum, b)
                nc.vector.tensor_copy(zt[:, TC * P:TC * P + 1], ps_sum).then_inc(sumx_ready, 1)

            def transpose_gram(b):
                dve.wait_ge(gram_ready, 4 * b + 4)
                wait(dve, zk_psum, b)
                nc.vector.transpose(zt[:, 0:TC * P], gram[:, :, :].rearrange("p q g -> p (q g)")).then_inc(zt_ready, 1)
                dve.wait_ge(zt_ready, b + 1)
                blocks_of_8 = pair_slices(zt)
                nc.vector.tensor_copy(zc[:, 0, :].rearrange("s (q p) -> s q p", q=8), blocks_of_8[0])
                nc.vector.tensor_copy(zc[:, 1, :].rearrange("s (q p) -> s q p", q=8), blocks_of_8[1])
                nc.vector.tensor_copy(zc[:, 2, :].rearrange("s (a q p) -> s a q p", a=2, q=8),
                                      blocks_of_8[2]).then_inc(zc_ready, 1)

            def stats_z(b):
                dve.wait_ge(z_psum, b + 1)
                nc.vector.bn_stats(stats[:, :], ps_a[:, :]).then_inc(stats_ready, 1)
                dve.wait_ge(stats_ready, b + 1)
                dve.nop(nofuse=True)
                nc.vector.bn_aggr(mv[:, :], stats[:, :]).then_inc(mv_ready, 1)

            def shift_z(b):
                dve.wait_ge(zstd_ready, b + 1)
                wait(dve, z_ready, b)
                nc.vector.reciprocal(zrstd[:, :], zstd[:, :]).then_inc(zrstd_ready, 1)
                dve.wait_ge(zrstd_ready, b + 1)
                nc.vector.tensor_scalar(zshift[:, :], zrstd[:, :], mv[:, 0:1], -1.0, ALU.mult,
                                        ALU.mult).then_inc(zshift_ready, 1)

            done = [0]

            def link(instruction):
                done[0] += 1
                instruction.then_inc(prep_dve, 1)
                dve.wait_ge(prep_dve, done[0])

            nc.vector.memset(proj[:, :, :], 0.0)
            nc.vector.memset(gram_w[:, :], 0.0)
            nc.vector.memset(half_ones[:, :], 0.0)
            nc.vector.memset(mean_ones[:, :], 1.0 / E)
            nc.vector.memset(ones[:, :], 1.0)
            nc.vector.memset(eps[:, :], EPS)
            nc.vector.memset(zt[:, TC * P + 1:TC * P + 2], 1.0)
            nc.vector.memset(v[0][:, :, P + 1], 1.0)
            nc.vector.memset(v[1][:, :, P + 1], 1.0)
            link(nc.vector.memset(fold[:, :, :], 0.0))
            assert done[0] == DVE_CONST
            nc.vector.memset(half_ones[0:D, 0:1], 1.0 / E)
            nc.vector.memset(half_ones[D:2 * D, 1:2], 1.0 / E)
            dve.wait_ge(interaction_w_in, 9 * DMA)
            link(nc.vector.tensor_reduce(wc_mean[:, :], wc[:, :], AX.X, ALU.add))
            link(nc.vector.tensor_scalar(wc_mean[:, :], wc_mean[:, :], 1.0 / E, None, ALU.mult))
            link(nc.vector.tensor_scalar(wc[:, :], wc[:, :], wc_mean[:, 0:1], None, ALU.subtract))
            assert done[0] == DVE_WC
            link(nc.vector.tensor_tensor(wcg[:, :], wc[:, :], gs_b[:, :], ALU.mult))
            dve.wait_ge(prep_pe, PE_GRAM)
            nc.vector.tensor_copy(gram_w[0:D, 0:D], ps_a[0:D, 0:D])
            link(nc.vector.tensor_copy(gram_w[D:2 * D, D:2 * D], ps_a[D:2 * D, D:2 * D]))
            assert done[0] == DVE_GRAM
            link(nc.vector.tensor_reduce(proj_mean[:, :], proj[:, :, :], AX.X, ALU.add))
            link(nc.vector.tensor_scalar(proj_mean[:, :], proj_mean[:, :], 1.0 / P, None, ALU.mult))
            link(nc.vector.tensor_tensor(proj[:, :, :], proj[:, :, :],
                                         proj_mean[:, :].unsqueeze(2).to_broadcast([ROWS, J, P]), ALU.subtract))
            assert done[0] == DVE_PROJ
            dve.wait_ge(x_w_in, 3 * DMA)
            link(nc.vector.tensor_reduce(wd_mean[:, :], wd[:, :, :], AX.X, ALU.add))
            link(nc.vector.scalar_tensor_tensor(
                wd[:, :, :], wd_mean[:, :].unsqueeze(2).to_broadcast([128, DK, E]), -1.0 / E, wd[:, :, :],
                ALU.mult, ALU.add))
            assert done[0] == DVE_WD
            quad_form(0, 0)
            scale_emb(0, 0, 0)
            quad_form(1, 1)
            dve.wait_ge(prep_pe, PE_YBIAS)
            link(nc.vector.tensor_copy(y_bias[:, :], ps_y[:, 0:P]))
            assert done[0] == DVE_YBIAS
            scale_x(0)
            finish_x(0)
            scale_emb(1, 1, 1)
            quad_form(2, 0)

            def fold_weights():
                dve.wait_ge(wl_in, 7 * DMA)
                a = coef[:, :, :]
                nc.vector.tensor_tensor(a[:, 0], bq[:, :], gp[:, :], ALU.mult)
                nc.vector.tensor_tensor(a[:, 1], bp[:, :], gq[:, :], ALU.mult)
                nc.vector.tensor_tensor(a[:, 2], gp[:, :], gq[:, :], ALU.mult)
                link(nc.vector.tensor_tensor(a[:, 3], bp[:, :], bq[:, :], ALU.mult))
                link(nc.vector.tensor_tensor(fold_q[:, :, :], isq[:, 0:KP, :],
                                             a[:, 1, 0:KP].unsqueeze(2).to_broadcast([128, KP, P]), ALU.mult))
                link(nc.vector.tensor_tensor(fold[:, 0:KP, P:2 * P], isp[:, 0:KP, :],
                                             a[:, 0, 0:KP].unsqueeze(2).to_broadcast([128, KP, P]), ALU.mult))
                link(nc.vector.tensor_tensor(fold[:, 0:KP, P:2 * P], fold[:, 0:KP, P:2 * P], fold_q[:, :, :], ALU.add))
                nc.vector.tensor_scalar(fold[:, 0:KP, KL - 1], a[:, 3, 0:KP], float(E), None, ALU.mult)
                nc.vector.tensor_copy(fold[0:P, KP, KL - 2:KL - 1], bp[0:P, KP:KP + 1])
                link(nc.vector.tensor_scalar(fold[0:P, KP, 0:P], isp[0:P, KP, :], gp[0:P, KP:KP + 1], None, ALU.mult))
                assert done[0] == DVE_FOLD
                dve.wait_ge(prep_pe, PE_FOLD)
                link(nc.vector.tensor_tensor(wl[:, 0:KP, :], wl[:, 0:KP, :],
                                             a[:, 2, 0:KP].unsqueeze(2).to_broadcast([128, KP, MAXD]), ALU.mult))
                dve.wait_ge(prep_pe, PE_B1)
                link(nc.vector.tensor_tensor(b1_f[:, :], ps_b[:, 0:H1 // 128], b1_c[:, :], ALU.add))
                assert done[0] == DVE_WL
                for kt in range(ZK - 1):
                    nc.vector.tensor_scalar(w1_s[:, kt, :], w1_s[:, kt, :], gl_c[:, kt:kt + 1], None, ALU.mult)
                link(nc.vector.tensor_scalar(w1_s[:, ZK - 1, :], w1_s[:, ZK - 1, :], gl_c[:, ZK - 1:ZK], None, ALU.mult))
                assert done[0] == DVE_W1

            def body(b, first, last):
                b2 = not isinstance(b, int) or b >= 2
                for k in range(STEPS):
                    i = 4 * b + k
                    bias_y(i, 0)
                    bias_y(i, 1)
                    if k == 1 and not first:
                        transpose_gram(b - 1)
                    if k == 2:
                        copy_sumx(b)
                    sum_squares(i)
                    if not (last and k >= 2):
                        scale_emb(i + 2, (k + 2) % STEPS, k % 2)
                    normalise_y(i, b, k, k % 2)
                    if k == 0 and not last:
                        scale_x(b + 1)
                    if k == 2 and not first:
                        stats_z(b - 1)
                        shift_z(b - 1)
                    if k == 3 and not last:
                        finish_x(b + 1)
                    if not (last and k >= 1):
                        quad_form(i + 3, (k + 1) % 2)
                if first:
                    fold_weights()

            blocks(dve, body)
            transpose_gram(NBLK - 1)
            stats_z(NBLK - 1)
            shift_z(NBLK - 1)

        @block.tensor
        def _(pe):
            mm = nc.tensor.matmul

            def transpose_emb(s, b, k):
                pe.wait_ge(gathered[k], GA * DMA * (b + 1))
                wait(pe, emb_t_ready, s)
                for t in range(PAIRS):
                    last = nc.tensor.transpose(ps_t[:, t * ROWS:(t + 1) * ROWS],
                                               emb[k][:, 2 * t:2 * t + 2, :].rearrange("r g d -> r (g d)"),
                                               ident[0:ROWS, 0:ROWS])
                last.then_inc(emb_t_psum, 1)

            def apply_gram_w(s, par):
                pe.wait_ge(emb_t_ready, s + 1)
                wait(pe, std_ready, s)
                mm(ps_q[:, 0:PAIRS * ROWS], gram_w[:, :], emb_t[par][:, :], start=True, stop=True).then_inc(q_psum, 1)

            def variances(s, par):
                pe.wait_ge(quad_ready, s + 1)
                for t in range(PAIRS):
                    last = mm(ps_q[0:ROWS, var_at + 2 * t:var_at + 2 * t + 2], quad[par][:, t * ROWS:(t + 1) * ROWS],
                              half_ones[:, :], start=True, stop=True)
                last.then_inc(var_psum, 1)

            def project(s, par):
                pe.wait_ge(emb_r_ready, s + 1)
                wait(pe, mix_ready, s)
                for t in range(PAIRS):
                    last = mm(ps_m[:, t * 128:(t + 1) * 128],
                              emb_r[par][:, 2 * t:2 * t + 2, :].rearrange("r g d -> r (g d)"),
                              proj[:, :, :].rearrange("r j p -> r (j p)"), start=True, stop=True)
                last.then_inc(mix_psum, 1)

            def expand(s, par):
                pe.wait_ge(mix_ready, s + 1)
                for h in range(2):
                    wait(pe, y_ready, 2 * s - 1 + h)
                    mm(ps_y[:, h * 512:(h + 1) * 512], wcg[h * D:(h + 1) * D, :], mix[par][h * D:(h + 1) * D, :],
                       start=True, stop=True).then_inc(y_psum, 1)

            def gram_v(s, par):
                pe.wait_ge(v_ready, s + 1)
                wait(pe, gram_ready, s)
                for g in range(GA):
                    c = (g % 2) * (SPS // 2) + (g // 2) * J
                    for j in range(J):
                        last = mm(ps_z[32 * j:32 * j + 32, g * TC:(g + 1) * TC], v[par][:, c + j, 0:P],
                                  v[par][:, c + j, :], start=True, stop=True)
                last.then_inc(gram_psum, 1)

            def project_x(b):
                pe.wait_ge(dense_x_in, DMA * (b + 1))
                wait(pe, x_scaled_ready, b)
                wait(pe, z_t_ready, b - 2)
                for kt in range(DK):
                    last = mm(ps_x, wd[:, kt, :], dense_x[:, kt, :], start=(kt == 0), stop=(kt == DK - 1))
                last.then_inc(x_psum, 1)

            def variance_x(b):
                pe.wait_ge(xsq_ready, b + 1)
                mm(ps_xv, mean_ones[:, :], xsq[:, :], start=True, stop=True).then_inc(xvar_psum, 1)

            def sum_x(b):
                pe.wait_ge(x_ready, b + 1)
                mm(ps_sum, x[:, :], ones[:, :], start=True, stop=True).then_inc(sumx_psum, 1)

            def transpose_z_pairs(b, x_blocks):
                pe.wait_ge(zc_ready, b + 1)
                pe.wait_ge(x_scaled_ready, x_blocks)
                wait(pe, score_ready, b)
                for t in range(4):
                    src = zt[:, t * 128:(t + 1) * 128] if t < 2 else zc[:, t - 2, :]
                    nc.tensor.transpose(ps_a[:, t * BLK:(t + 1) * BLK], src, ident[:, :])
                nc.tensor.transpose(ps_b[:, 0:BLK], zc[:, 2, :], ident[:, :])
                nc.tensor.transpose(ps_b[0:KL, BLK:2 * BLK], zt[:, P * P:P * P + KL], ident[:, :]).then_inc(zk_psum, 1)

            def z_first(b):
                pe.wait_ge(zk_ready, b + 1)
                for t in range(3):
                    mm(ps_a[:, :], zk[:, t, :], wl[:, t, :], start=(t == 0), stop=False)

            def z_second(b):
                for t in range(3, KP):
                    mm(ps_a[:, :], zk[:, t, :], wl[:, t, :], start=False, stop=False)
                mm(ps_a[:, :], zk[0:KL, KP, :], wl[0:KL, KP, :], start=False, stop=True).then_inc(z_psum, 1)

            def transpose_z(b, x_blocks):
                pe.wait_ge(z_ready, b + 1)
                pe.wait_ge(sumx_ready, x_blocks)
                for t in range(ZK):
                    last = nc.tensor.transpose(ps_b[:, t * BLK:(t + 1) * BLK], z[:, t * 128:(t + 1) * 128], ident[:, :])
                last.then_inc(z_t_psum, 1)

            def top1(b, half):
                if half == 0:
                    pe.wait_ge(z_t_ready, b + 1)
                    pe.wait_ge(dense_h_in, DMA * (b + 1))
                for m in range(half * 2, half * 2 + 2):
                    for kt in range(ZK + DK):
                        rhs = z_t[:, kt, :] if kt < ZK else dense_h[:, kt - ZK, :]
                        last = mm(ps_a[:, m * BLK:(m + 1) * BLK], w1_s[:, kt, m * 128:(m + 1) * 128], rhs,
                                  start=(kt == 0), stop=(kt == ZK + DK - 1))
                if half == 1:
                    last.then_inc(h1_psum, 1)

            def top2(b):
                pe.wait_ge(h1_ready, b + 1)
                n = H1 // 128
                for m in range(H2 // 128):
                    for kt in range(n):
                        last = mm(ps_a[:, m * BLK:(m + 1) * BLK], w2_s[:, kt, m * 128:(m + 1) * 128], h1[:, kt, :],
                                  start=(kt == 0), stop=(kt == n - 1))
                last.then_inc(h2_psum, 1)

            def top3(b):
                pe.wait_ge(h2_ready, b + 1)
                n = H2 // 128
                for kt in range(n):
                    last = mm(ps_a[0:1, 256:384], w3_s[:, kt:kt + 1], h2[:, kt, :], start=(kt == 0), stop=(kt == n - 1))
                last.then_inc(score_psum, 1)

            pe.wait_ge(prep_dve, DVE_WC)
            nc.tensor.transpose(ps_a[:, 0:2 * D], wc[:, :], ident[:, :]).then_inc(prep_pe, 1)
            pe.wait_ge(prep_act, ACT_WCE)
            mm(ps_a[:, 0:2 * D], wc_e[:, :], wc_e[:, :], start=True, stop=True).then_inc(prep_pe, 1)
            pe.wait_ge(prep_dve, DVE_PROJ)
            mm(ps_y[:, 0:P], bs_b[:, :], proj[0:NF, 0, :], start=True, stop=True).then_inc(prep_pe, 1)
            pe.wait_ge(prep_dve, DVE_WD)
            project_x(0)
            transpose_emb(0, 0, 0)
            apply_gram_w(0, 0)
            transpose_emb(1, 0, 1)
            variances(0, 0)
            variance_x(0)
            apply_gram_w(1, 1)
            project(0, 0)
            transpose_emb(2, 0, 2)
            variances(1, 1)
            apply_gram_w(2, 0)
            pe.wait_ge(prep_dve, DVE_YBIAS)

            def body(b, first, last):
                b2 = not isinstance(b, int) or b >= 2
                for k in range(STEPS):
                    i = 4 * b + k
                    expand(i, k % 2)
                    if not (last and k >= 2):
                        variances(i + 2, k % 2)
                    if k == 0:
                        if b2:
                            top2(b - 2)
                        if not last:
                            project_x(b + 1)
                    if k == 2 and not first:
                        z_second(b - 1)
                    if k == 3 and not first:
                        top1(b - 1, 0)
                    if not (last and k >= 1):
                        transpose_emb(i + 3, b + (k + 3) // STEPS, (k + 3) % STEPS)
                    if not (last and k == 3):
                        project(i + 1, (k + 1) % 2)
                    if k == 0:
                        if b2:
                            top3(b - 2)
                        if not last:
                            variance_x(b + 1)
                    if k == 1 and not first:
                        transpose_z_pairs(b - 1, NBLK if last else b + 2)
                    if not (first and k == 0):
                        gram_v(i - 1, (k + 1) % 2)
                    if not (last and k >= 1):
                        apply_gram_w(i + 3, (k + 1) % 2)
                    if k == 1:
                        if not first:
                            z_first(b - 1)
                        sum_x(b)
                    if k == 2 and not first:
                        transpose_z(b - 1, b + 1)
                    if k == 3 and not first:
                        top1(b - 1, 1)
                if first:
                    pe.wait_ge(prep_dve, DVE_FOLD)
                    for t in range(KP):
                        mm(ps_a[0:KL, :], fold[:, t, :], wl[:, t, :], start=(t == 0), stop=False)
                    mm(ps_a[0:KL, :], fold[0:P, KP, :], wl[0:P, KP, :], start=False, stop=True).then_inc(prep_pe, 1)
                    pe.wait_ge(sumx_ready, 1)
                    pe.wait_ge(x_scaled_ready, 2)
                    pe.wait_ge(mlp_w_in, 7 * DMA)
                    for m in range(H1 // 128):
                        for kt in range(ZK):
                            last = mm(ps_b[:, m:m + 1], w1_s[:, kt, m * 128:(m + 1) * 128], bl_c[:, kt:kt + 1],
                                      start=(kt == 0), stop=(kt == ZK - 1))
                    last.then_inc(prep_pe, 1)
                    pe.wait_ge(prep_dve, DVE_W1)
                    pe.wait_ge(prep_act, ACT_FOLD)

            blocks(pe, body)
            b = NBLK - 1
            gram_v(NS - 1, (NS - 1) % 2)
            top2(b - 1)
            top3(b - 1)
            transpose_z_pairs(b, NBLK)
            z_first(b)
            z_second(b)
            transpose_z(b, NBLK)
            top1(b, 0)
            top1(b, 1)
            top2(b)
            top3(b)


def kernel(**inputs):
    import numpy as np
    import concourse.bacc as bacc
    from concourse.bass_utils import run_bass_kernel_spmd

    def f(name):
        return np.asarray(inputs[name])

    tables = [f(f"tbl_{n}") for n in range(NF)]
    base = np.cumsum([0] + [t.shape[0] for t in tables[:-1]]).astype(np.int32)
    tiles = pair_tiles()
    wl = f("L0_rec_Wl")
    gsi, bsi = f("L0_rec_gsi"), f("L0_rec_bsi")
    wl_pairs = np.zeros((128, KP + 1, MAXD), wl.dtype)
    of_p = np.zeros((128, KP + 1), np.int64)
    of_q = np.zeros((128, KP + 1), np.int64)
    is_p = np.zeros((128, KP + 1, P), np.float32)
    is_q = np.zeros((128, KP + 1, P), np.float32)
    for t, rows in enumerate(tiles):
        for r, (q, p) in enumerate(rows):
            of_p[r, t], of_q[r, t] = p, q
            is_p[r, t, p] = is_q[r, t, q] = 1.0
            if p > q:
                wl_pairs[r, t] = wl[:, (p + 1) * p // 2 + q + 1]
    for p in range(P):
        of_p[p, KP] = p
        is_p[p, KP, p] = 1.0
        wl_pairs[p, KP] = wl[:, (p + 1) * p // 2]

    def columns(a):
        return np.ascontiguousarray(a.reshape(-1, 128).T)

    def k_tiles(a):
        return np.ascontiguousarray(a.reshape(-1, 128, a.shape[1]).transpose(1, 0, 2))

    w1 = f("W_top1")
    arrays = {
        "dense_t": k_tiles(f("r_dense_t").T),
        "ids": np.ascontiguousarray(f("ids").reshape(NBLK, J, STEPS * GA, NF).transpose(1, 3, 0, 2).reshape(ROWS, -1)),
        "row_base": np.tile(base, J).reshape(ROWS, 1),
        "tables": np.concatenate(tables, axis=0),
        "ws_t": np.ascontiguousarray(f("L0_rec_Ws").T),
        "gs": f("L0_rec_gs"),
        "bs": f("L0_rec_bs"),
        "wsi_t": np.ascontiguousarray(f("L0_rec_Wsi").T),
        "wd_t": k_tiles(f("L0_rec_Wd").T),
        "gd": columns(f("L0_rec_gd")),
        "bd": columns(f("L0_rec_bd")),
        "wl_pairs": wl_pairs,
        "g_of_p": gsi[of_p],
        "g_of_q": gsi[of_q],
        "b_of_p": bsi[of_p],
        "b_of_q": bsi[of_q],
        "is_p": is_p,
        "is_q": is_q,
        "gsi": gsi,
        "identity": np.eye(128, dtype=np.float32),
        "gl": columns(f("L0_rec_gl")[:DIMS]),
        "bl": columns(f("L0_rec_bl")[:DIMS]),
        "w1": k_tiles(np.concatenate([w1[:DIMS], w1[MAXD:]], axis=0)),
        "b1": columns(f("b_top1")),
        "w2": k_tiles(f("W_top2")),
        "b2": columns(f("b_top2")),
        "w3": columns(f("W_top3").reshape(-1)),
    }
    nc = bacc.Bacc("TRN2", target_bir_lowering=False, num_devices=1)
    args = [nc.dram_tensor(f"in_{name}", a.shape, mybir.dt.from_np(a.dtype), kind="ExternalInput").ap()
            for name, a in arrays.items()]
    out = nc.dram_tensor("scores", (1, B), F32, kind="ExternalOutput").ap()
    dlrm_kernel(nc, *args, out)
    r = run_bass_kernel_spmd(nc, [{f"in_{name}": a for name, a in arrays.items()}], core_ids=[0])
    return r.results[0]["scores"].reshape(B, 1)
```

```python
import concourse.bass as bass
from concourse import mybir
from contextlib import ExitStack

F32 = mybir.dt.float32
I32 = mybir.dt.int32
ALU = mybir.AluOpType
ACT = mybir.ActivationFunctionType
AX = mybir.AxisListType

B, DENSE, NF, D, E, P = 2048, 256, 26, 64, 128, 32
MAXD, DIMS = 512, 384
H1, H2 = 512, 256
EPS = 1e-5
BLK = 128
NBLK = B // BLK
STEPS = 4
J = 4
ROWS = J * NF
GA = 8
SPS = J * GA
PAIRS = GA // 2
TC = P + 2
NS = NBLK * STEPS
SIDE = 2 * P + 2
SIDE_AT = 512
SIDE_END = SIDE_AT + SIDE
ZROWS = SIDE_END + 9
KT = 5
KL = ZROWS - 128 * (KT - 1)
ZK = DIMS // 128
DK = DENSE // 128
DMA = 16


def pair_order():
    order = [(q, q + 1 + c) for q in range(16) for c in range(16)]
    order += [(16 * t + q, 17 + q + c) for t in range(2) for q in range(8) for c in range(8)]
    order += [(8 * t + q, 25 + q + c) for t in range(4) for q in range(4) for c in range(4)]
    order += [(4 * t + q, 29 + c) for t in range(8) for q in range(3) for c in range(3)]
    return [(r if r < 511 else r - 511 + SIDE_END, q, p) for r, (q, p) in enumerate(order)]


def pair_pieces(zt, packed):
    def bands(triangles, start, rows, width):
        part = zt[:, 0:P * P].rearrange("s (t m) -> s t m", t=triangles)[:, :, start:start + rows * (P + 1)]
        return part.rearrange("s t (q c) -> s t q c", c=P + 1)[:, :, :, 0:width]

    def at(first, last, triangles, width):
        return packed[:, first:last].rearrange("s (t q c) -> s t q c", t=triangles, c=width)

    corners = zt[:, 0:P * P].rearrange("s (t q p) -> s t q p", t=8, p=P)[:, :, 0:3, P - 3:P]
    return [(at(0, 256, 1, 16)[:, 0], bands(1, 1, 16, 16)[:, 0]),
            (at(256, 384, 2, 8), bands(2, 17, 8, 8)),
            (at(384, 448, 4, 4), bands(4, 25, 4, 4)),
            (at(448, 511, 7, 3), corners[:, 0:7]),
            (at(SIDE_END, SIDE_END + 9, 1, 3)[:, 0], corners[:, 7])]


def dlrm_kernel(nc, dense_t, ids, row_base, tables, ws_t, gs, bs, wsi_t, wd_t, gd, bd, wl_pairs,
                g_of_p, g_of_q, b_of_p, b_of_q, is_p, is_q, identity, gl, bl, w1, b1, w2, b2, w3, out):
    ctx = ExitStack()

    def sb(name, shape, dt=F32):
        return ctx.enter_context(nc.sbuf_tensor(name, shape, dt))

    def pb(name, shape):
        return ctx.enter_context(nc.psum_tensor(name, shape, F32))

    def sem(name):
        return ctx.enter_context(nc.semaphore(name))

    with ctx:
        ident = sb("ident", [128, 128])
        feature_id = sb("feature_id", [ROWS, NBLK * STEPS * GA], I32)
        rows = [sb(f"rows{k}", [ROWS, GA], I32) for k in range(STEPS)]
        base = sb("base", [ROWS, 1], I32)
        wc = sb("wc", [2 * D, E])
        wcg = sb("wcg", [2 * D, E])
        wc_e = sb("wc_e", [E, 2 * D])
        gram_w = sb("gram_w", [2 * D, 2 * D])
        proj = sb("proj", [ROWS, J, P])
        proj_mean = sb("proj_mean", [ROWS, J])
        gs_b = sb("gs_b", [2 * D, E])
        bs_b = sb("bs_b", [NF, E])
        y_bias = sb("y_bias", [E, P])
        wd = sb("wd", [128, DK, E])
        wd_mean = sb("wd_mean", [128, DK])
        wc_mean = sb("wc_mean", [2 * D, 1])
        gd_c = sb("gd_c", [E, 1])
        bd_c = sb("bd_c", [E, 1])
        mean_ones = sb("mean_ones", [E, E])
        ones = sb("ones", [E, 1])
        wl = sb("wl", [128, KT, MAXD])
        gp = sb("gp", [128, KT])
        gq = sb("gq", [128, KT])
        bp = sb("bp", [128, KT])
        bq = sb("bq", [128, KT])
        isp = sb("isp", [128, KT, P])
        isq = sb("isq", [128, KT, P])
        coef = sb("coef", [128, 4, KT])
        fold = sb("fold", [128, KT, SIDE])
        fold_q = sb("fold_q", [128, KT, P])
        w1_s = sb("w1_s", [128, ZK + DK, H1])
        gl_c = sb("gl_c", [128, ZK])
        bl_c = sb("bl_c", [128, ZK])
        b1_c = sb("b1_c", [128, H1 // 128])
        b1_f = sb("b1_f", [128, H1 // 128])
        w2_s = sb("w2_s", [128, H1 // 128, H2])
        b2_c = sb("b2_c", [128, H2 // 128])
        w3_s = sb("w3_s", [128, H2 // 128])
        emb = [sb(f"emb{k}", [ROWS, GA, D]) for k in range(STEPS)]
        emb_t = [sb(f"emb_t{i}", [2 * D, PAIRS * ROWS]) for i in range(2)]
        quad = sb("quad", [ROWS, GA, D])
        var = sb("var", [ROWS, GA])
        eps = sb("eps", [128, 1])
        std = sb("std", [ROWS, GA])
        rstd = sb("rstd", [ROWS, GA])
        emb_r = [sb(f"emb_r{i}", [ROWS, GA, D]) for i in range(2)]
        mix = [sb(f"mix{i}", [2 * D, PAIRS * J * P]) for i in range(2)]
        y = sb("y", [E, SPS, P])
        ysq = sb("ysq", [E, SPS, P])
        yvar = sb("yvar", [E, SPS])
        ystd = sb("ystd", [E, SPS])
        yrstd = sb("yrstd", [E, SPS])
        v = [sb(f"v{i}", [E, SPS, TC]) for i in range(2)]
        dense_x = sb("dense_x", [128, DK, BLK])
        dense_h = sb("dense_h", [128, DK, BLK])
        xsq = sb("xsq", [E, BLK])
        xstd = sb("xstd", [E, BLK])
        xrstd = sb("xrstd", [E, BLK])
        x_scaled = sb("x_scaled", [E, BLK])
        x = sb("x", [E, BLK])
        gram = sb("gram", [128, TC, BLK // J])
        zt = sb("zt", [BLK, P * P])
        zc = sb("zc", [BLK, ZROWS])
        zk = sb("zk", [128, KT, BLK])
        stats = sb("stats", [BLK, 6])
        mv = sb("mv", [BLK, 2])
        zstd = sb("zstd", [BLK, 1])
        zrstd = sb("zrstd", [BLK, 1])
        zshift = sb("zshift", [BLK, 1])
        z = sb("z", [BLK, DIMS])
        z_t = sb("z_t", [128, ZK, BLK])
        h1 = sb("h1", [128, H1 // 128, BLK])
        h2 = sb("h2", [128, H2 // 128, BLK])
        score = sb("score", [1, BLK])
        ps_t = pb("ps_t", [128, 512])
        ps_q = pb("ps_q", [128, 512])
        ps_m = pb("ps_m", [128, 512])
        ps_y = pb("ps_y", [128, 1024])
        ps_z = pb("ps_z", [128, 512])
        ps_a = pb("ps_a", [128, 512])
        ps_b = pb("ps_b", [128, 512])
        ps_sum = ps_b[:, 0:1]
        ps_x = ps_b[:, 384:512]
        ps_xv = ps_b[:, 256:384]

        ids_in = sem("ids_in")
        interaction_w_in = sem("interaction_w_in")
        x_w_in = sem("x_w_in")
        wl_in = sem("wl_in")
        mlp_w_in = sem("mlp_w_in")
        dense_x_in = sem("dense_x_in")
        dense_h_in = sem("dense_h_in")
        gathered = [sem(f"gathered{k}") for k in range(STEPS)]
        out_done = sem("out_done")
        prep_dve = sem("prep_dve")
        prep_pe = sem("prep_pe")
        prep_act = sem("prep_act")
        rows_ready = sem("rows_ready")
        emb_t_psum = sem("emb_t_psum")
        emb_t_ready = sem("emb_t_ready")
        q_psum = sem("q_psum")
        quad_ready = sem("quad_ready")
        var_ready = sem("var_ready")
        std_ready = sem("std_ready")
        rstd_ready = sem("rstd_ready")
        emb_r_ready = sem("emb_r_ready")
        mix_psum = sem("mix_psum")
        mix_ready = sem("mix_ready")
        y_psum = sem("y_psum")
        y_ready = sem("y_ready")
        ysq_ready = sem("ysq_ready")
        yvar_ready = sem("yvar_ready")
        ystd_ready = sem("ystd_ready")
        yrstd_ready = sem("yrstd_ready")
        v_ready = sem("v_ready")
        gram_psum = sem("gram_psum")
        gram_ready = sem("gram_ready")
        x_psum = sem("x_psum")
        xsq_ready = sem("xsq_ready")
        xvar_psum = sem("xvar_psum")
        xstd_ready = sem("xstd_ready")
        xrstd_ready = sem("xrstd_ready")
        x_scaled_ready = sem("x_scaled_ready")
        x_ready = sem("x_ready")
        sumx_psum = sem("sumx_psum")
        sumx_ready = sem("sumx_ready")
        zt_ready = sem("zt_ready")
        zc_ready = sem("zc_ready")
        zk_psum = sem("zk_psum")
        zk_ready = sem("zk_ready")
        z_psum = sem("z_psum")
        stats_ready = sem("stats_ready")
        mv_ready = sem("mv_ready")
        zstd_ready = sem("zstd_ready")
        zrstd_ready = sem("zrstd_ready")
        zshift_ready = sem("zshift_ready")
        z_ready = sem("z_ready")
        z_t_psum = sem("z_t_psum")
        z_t_ready = sem("z_t_ready")
        h1_psum = sem("h1_psum")
        h1_ready = sem("h1_ready")
        h2_psum = sem("h2_psum")
        h2_ready = sem("h2_ready")
        score_psum = sem("score_psum")
        score_ready = sem("score_ready")

        DVE_CONST, DVE_WC, DVE_GRAM, DVE_PROJ, DVE_WD, DVE_YBIAS, DVE_FOLD, DVE_WL, DVE_B1, DVE_W1 = 1, 4, 6, 9, 11, 12, 17, 18, 19, 20
        PE_WCE, PE_GRAM, PE_YBIAS, PE_FOLD, PE_B1 = 1, 2, 3, 4, 5
        ACT_WCE, ACT_FOLD = 1, 2

        def wait(engine, semaphore, count):
            if not isinstance(count, int) or count > 0:
                engine.wait_ge(semaphore, count)

        def blocks(engine, body):
            body(0, True, False)
            body(1, False, False)
            with engine.Fori(2, NBLK - 1) as b:
                body(b, False, False)
            body(NBLK - 1, False, True)

        block = ctx.enter_context(nc.Block())

        @block.sync
        def _(sp):
            sp.dma_start(feature_id[:, :], ids).then_inc(ids_in, DMA)
            sp.dma_start(base[:, :], row_base).then_inc(ids_in, DMA)
            sp.dma_start(dense_x[:, :, :], dense_t[:, :, 0:BLK]).then_inc(dense_x_in, DMA)
            sp.dma_start(wd[:, :, :], wd_t).then_inc(x_w_in, DMA)
            sp.dma_start(gd_c[:, :], gd).then_inc(x_w_in, DMA)
            sp.dma_start(bd_c[:, :], bd).then_inc(x_w_in, DMA)
            sp.dma_start(w1_s[:, :, :], w1).then_inc(mlp_w_in, DMA)
            sp.dma_start(w2_s[:, :, :], w2).then_inc(mlp_w_in, DMA)
            sp.dma_start(w3_s[:, :], w3).then_inc(mlp_w_in, DMA)
            sp.dma_start(gl_c[:, :], gl).then_inc(mlp_w_in, DMA)
            sp.dma_start(bl_c[:, :], bl).then_inc(mlp_w_in, DMA)
            sp.dma_start(b1_c[:, :], b1).then_inc(mlp_w_in, DMA)
            sp.dma_start(b2_c[:, :], b2).then_inc(mlp_w_in, DMA)

            def dense_for_x(b):
                sp.wait_ge(x_psum, b)
                sp.dma_start(dense_x[:, :, :], dense_t[:, :, bass.ds(b * BLK, BLK)]).then_inc(dense_x_in, DMA)

            def body(b, first, last):
                if first:
                    dense_for_x(1)
                if not last:
                    dense_for_x(b + 2)
                wait(sp, h1_psum, b)
                sp.dma_start(dense_h[:, :, :], dense_t[:, :, bass.ds(b * BLK, BLK)]).then_inc(dense_h_in, DMA)
                if not first:
                    sp.wait_ge(score_ready, b)
                    sp.dma_start(out[:, bass.ds((b - 1) * BLK, BLK)], score[:, :]).then_inc(out_done, DMA)

            body(0, True, False)
            with sp.Fori(1, NBLK - 2) as b:
                body(b, False, False)
            body(NBLK - 2, False, True)
            body(NBLK - 1, False, True)
            sp.wait_ge(score_ready, NBLK)
            sp.dma_start(out[:, (NBLK - 1) * BLK:B], score[:, :]).then_inc(out_done, DMA)
            sp.wait_ge(out_done, DMA * NBLK)

        @block.gpsimd
        def _(pool):
            pool.wait_ge(ids_in, 2 * DMA)

            def body(b, first, last):
                for k in range(STEPS):
                    if not first:
                        pool.wait_ge(gathered[k], GA * DMA * b)
                    pool.tensor_tensor(rows[k][:, :], feature_id[:, bass.ds(b * (STEPS * GA) + k * GA, GA)],
                                       base[:, 0:1].to_broadcast([ROWS, GA]), ALU.add).then_inc(rows_ready, 1)
                    if not first:
                        pool.wait_ge(emb_r_ready, 4 * b - 3 + k)
                    pool.wait_ge(rows_ready, 4 * b + k + 1)
                    pool.nop(nofuse=True)
                    for g in range(GA):
                        pool.indirect_dma_start(
                            out=emb[k][:, g, :], out_offset=None, in_=tables,
                            in_offset=bass.IndirectOffsetOnAxis(ap=rows[k][:, g:g + 1], axis=0),
                        ).then_inc(gathered[k], DMA)

            blocks(pool, body)

        @block.scalar
        def _(act):
            act.dma_start(wc[0:D, :], ws_t).then_inc(interaction_w_in, DMA)
            act.dma_start(wc[D:2 * D, :], ws_t).then_inc(interaction_w_in, DMA)
            act.dma_start(ident[:, :], identity).then_inc(interaction_w_in, DMA)
            act.dma_start(gs_b[:, :], gs.partition_broadcast(2 * D)).then_inc(interaction_w_in, DMA)
            act.dma_start(bs_b[:, :], bs.partition_broadcast(NF)).then_inc(interaction_w_in, DMA)
            act.wait_ge(prep_dve, DVE_CONST)
            for j in range(J):
                act.dma_start(proj[j * NF:(j + 1) * NF, j, :], wsi_t).then_inc(interaction_w_in, DMA)
            act.dma_start(wl[:, :, :], wl_pairs).then_inc(wl_in, DMA)
            for tile, source in ((gp, g_of_p), (gq, g_of_q), (bp, b_of_p), (bq, b_of_q)):
                act.dma_start(tile[:, :], source).then_inc(wl_in, DMA)
            act.dma_start(isp[:, :, :], is_p).then_inc(wl_in, DMA)
            act.dma_start(isq[:, :, :], is_q).then_inc(wl_in, DMA)

            def copy_emb_t(s, par):
                act.wait_ge(emb_t_psum, s + 1)
                wait(act, q_psum, s - 1)
                nc.scalar.copy(emb_t[par][:, :], ps_t[:, 0:PAIRS * ROWS]).then_inc(emb_t_ready, 1)

            def copy_mix(s, par):
                act.wait_ge(mix_psum, s + 1)
                wait(act, y_psum, 2 * s - 2)
                nc.scalar.copy(mix[par][:, :], ps_m[:, :]).then_inc(mix_ready, 1)

            def std_emb(s):
                act.wait_ge(var_ready, s + 1)
                wait(act, rstd_ready, s)
                nc.scalar.activation(std[:, :], var[:, :], ACT.Sqrt, bias=eps[0:ROWS, 0:1],
                                     scale=1.0 / E).then_inc(std_ready, 1)

            def std_y(s):
                act.wait_ge(yvar_ready, s + 1)
                wait(act, yrstd_ready, s)
                nc.scalar.activation(ystd[:, :], yvar[:, :], ACT.Sqrt, bias=eps[:, 0:1],
                                     scale=1.0 / P).then_inc(ystd_ready, 1)

            def std_x(b):
                act.wait_ge(xvar_psum, b + 1)
                wait(act, xrstd_ready, b)
                nc.scalar.activation(xstd[:, :], ps_xv, ACT.Sqrt, bias=eps[:, 0:1]).then_inc(xstd_ready, 1)

            def std_z(b):
                act.wait_ge(mv_ready, b + 1)
                wait(act, zrstd_ready, b)
                nc.scalar.activation(zstd[:, :], mv[:, 1:2], ACT.Sqrt, bias=eps[:, 0:1]).then_inc(zstd_ready, 1)

            def square_y(s, h):
                act.wait_ge(y_ready, 2 * s + 1 + h)
                if h == 0:
                    wait(act, yvar_ready, s)
                c = slice(h * SPS // 2, (h + 1) * SPS // 2)
                nc.scalar.activation(ysq[:, c, :], y[:, c, :], ACT.Square).then_inc(ysq_ready, 1)

            def copy_gram(s, b, k):
                act.wait_ge(gram_psum, s + 1)
                if k == 0:
                    wait(act, zc_ready, b)
                src = ps_z[:, 0:GA * TC].rearrange("p (g q) -> p q g", q=TC)
                nc.scalar.copy(gram[:, :, k * GA:(k + 1) * GA], src).then_inc(gram_ready, 1)

            def square_x(b):
                act.wait_ge(x_psum, b + 1)
                wait(act, xvar_psum, b)
                nc.scalar.activation(xsq[:, :], ps_x, ACT.Square).then_inc(xsq_ready, 1)

            def copy_zk(b):
                act.wait_ge(zk_psum, b + 1)
                wait(act, z_psum, b)
                nc.scalar.copy(zk[:, 0:4, :], ps_a[:, :].rearrange("p (t s) -> p t s", t=4))
                nc.scalar.copy(zk[0:KL, KT - 1, :], ps_b[0:KL, 0:BLK]).then_inc(zk_ready, 1)

            def normalise_z(b):
                act.wait_ge(zshift_ready, b + 1)
                wait(act, z_t_psum, b)
                nc.scalar.activation(z[:, :], ps_a[:, 0:DIMS], ACT.Identity, bias=zshift[:, 0:1],
                                     scale=zrstd[:, 0:1]).then_inc(z_ready, 1)

            def copy_z_t(b):
                act.wait_ge(z_t_psum, b + 1)
                wait(act, h1_psum, b)
                nc.scalar.copy(z_t[:, :, :], ps_b[:, 0:DIMS].rearrange("p (t s) -> p t s", t=ZK)).then_inc(z_t_ready, 1)

            def relu_h1(b):
                act.wait_ge(h1_psum, b + 1)
                wait(act, h2_psum, b)
                for m in range(H1 // 128):
                    last = nc.scalar.activation(h1[:, m, :], ps_a[:, m * BLK:(m + 1) * BLK], ACT.Relu,
                                                bias=b1_f[:, m:m + 1])
                last.then_inc(h1_ready, 1)

            def relu_h2(b):
                act.wait_ge(h2_psum, b + 1)
                wait(act, score_psum, b)
                for m in range(H2 // 128):
                    last = nc.scalar.activation(h2[:, m, :], ps_a[:, m * BLK:(m + 1) * BLK], ACT.Relu,
                                                bias=b2_c[:, m:m + 1])
                last.then_inc(h2_ready, 1)

            def copy_score(b):
                act.wait_ge(score_psum, b + 1)
                wait(act, out_done, DMA * b)
                nc.scalar.copy(score[:, :], ps_a[0:1, 256:384]).then_inc(score_ready, 1)

            act.wait_ge(prep_pe, PE_WCE)
            nc.scalar.copy(wc_e[:, :], ps_a[:, 0:2 * D]).then_inc(prep_act, 1)
            square_x(0)
            copy_emb_t(0, 0)
            copy_emb_t(1, 1)
            std_emb(0)
            std_x(0)
            copy_mix(0, 0)
            copy_emb_t(2, 0)
            std_emb(1)
            act.wait_ge(mlp_w_in, 7 * DMA)

            def body(b, first, last):
                b2 = not isinstance(b, int) or b >= 2
                for k in range(STEPS):
                    i = 4 * b + k
                    if k == 0 and b2:
                        relu_h1(b - 2)
                    square_y(i, 0)
                    if k == 3 and not first:
                        copy_z_t(b - 1)
                    square_y(i, 1)
                    if k == 1:
                        if not last:
                            copy_emb_t(i + 3, (k + 1) % 2)
                        copy_mix(i + 1, (k + 1) % 2)
                        if not first:
                            copy_zk(b - 1)
                    if not (last and k >= 2):
                        std_emb(i + 2)
                    if k == 0:
                        if b2:
                            relu_h2(b - 2)
                        if not last:
                            square_x(b + 1)
                    if k == 3:
                        std_y(i)
                    if k != 1 and not (last and k >= 1):
                        copy_emb_t(i + 3, (k + 1) % 2)
                    if k != 3:
                        std_y(i)
                    if k != 1 and not (last and k == 3):
                        copy_mix(i + 1, (k + 1) % 2)
                    if k == 0:
                        if b2:
                            copy_score(b - 2)
                        if not last:
                            std_x(b + 1)
                    if k == 2 and not first:
                        std_z(b - 1)
                    if k > 0:
                        copy_gram(i - 1, b, k - 1)
                    elif not first:
                        copy_gram(i - 1, b - 1, STEPS - 1)
                    if k == 2 and not first:
                        normalise_z(b - 1)
                if first:
                    act.wait_ge(prep_pe, PE_FOLD)
                    act.wait_ge(prep_dve, DVE_WL)
                    nc.scalar.copy(wl[0:SIDE, KT - 1, :], ps_a[0:SIDE, :]).then_inc(prep_act, 1)

            blocks(act, body)
            b = NBLK - 1
            relu_h1(b - 1)
            copy_gram(NS - 1, b, STEPS - 1)
            relu_h2(b - 1)
            copy_score(b - 1)
            copy_zk(b)
            std_z(b)
            normalise_z(b)
            copy_z_t(b)
            relu_h1(b)
            relu_h2(b)
            copy_score(b)

        @block.vector
        def _(dve):
            def quad_form(s, k):
                dve.wait_ge(q_psum, s + 1)
                wait(dve, var_ready, s)
                nc.vector.tensor_tensor(quad[:, :, :], ps_q[0:ROWS, :].rearrange("r (g d) -> r g d", d=D),
                                        emb[k][:, :, :], ALU.mult).then_inc(quad_ready, 1)

            def sum_quad(s):
                wait(dve, std_ready, s)
                dve.wait_ge(quad_ready, s + 1)
                nc.vector.tensor_reduce(var[:, :], quad[:, :, :], AX.X, ALU.add).then_inc(var_ready, 1)

            def scale_emb(s, k, par):
                dve.wait_ge(std_ready, s + 1)
                nc.vector.reciprocal(rstd[:, :], std[:, :]).then_inc(rstd_ready, 1)
                wait(dve, mix_psum, s - 1)
                dve.wait_ge(rstd_ready, s + 1)
                nc.vector.tensor_tensor(emb_r[par][:, :, :], emb[k][:, :, :],
                                        rstd[:, :].unsqueeze(2).to_broadcast([ROWS, GA, D]),
                                        ALU.mult).then_inc(emb_r_ready, 1)

            def bias_y(s, h):
                if h == 0:
                    wait(dve, v_ready, s)
                dve.wait_ge(y_psum, 2 * s + 1 + h)
                n = SPS // 2
                src = ps_y[:, h * 512:(h + 1) * 512].rearrange("e (s p) -> e s p", p=P)
                nc.vector.tensor_tensor(y[:, h * n:(h + 1) * n, :], src,
                                        y_bias[:, :].unsqueeze(1).to_broadcast([E, n, P]),
                                        ALU.add).then_inc(y_ready, 1)

            def sum_squares(s):
                dve.wait_ge(ysq_ready, 2 * s + 2)
                nc.vector.tensor_reduce(yvar[:, :], ysq[:, :, :], AX.X, ALU.add).then_inc(yvar_ready, 1)

            def normalise_y(s, b, k, par):
                wait(dve, gram_psum, s - 1)
                dve.wait_ge(x_ready, b + 1)
                xk = x[:, :].rearrange("e (j k t h) -> e k h t j", j=J, k=STEPS, h=2)[:, k]
                nc.vector.tensor_copy(v[par][:, :, P].rearrange("e (h t j) -> e h t j", h=2, j=J), xk)
                dve.wait_ge(ystd_ready, s + 1)
                nc.vector.reciprocal(yrstd[:, :], ystd[:, :]).then_inc(yrstd_ready, 1)
                dve.wait_ge(yrstd_ready, s + 1)
                nc.vector.tensor_tensor(v[par][:, :, 0:P], y[:, :, :],
                                        yrstd[:, :].unsqueeze(2).to_broadcast([E, SPS, P]),
                                        ALU.mult).then_inc(v_ready, 1)

            def scale_x(b):
                dve.wait_ge(xstd_ready, b + 1)
                nc.vector.reciprocal(xrstd[:, :], xstd[:, :]).then_inc(xrstd_ready, 1)
                dve.wait_ge(xrstd_ready, b + 1)
                nc.vector.tensor_tensor(x_scaled[:, :], ps_x, xrstd[:, :], ALU.mult).then_inc(x_scaled_ready, 1)

            def finish_x(b):
                dve.wait_ge(x_scaled_ready, b + 1)
                wait(dve, sumx_psum, b)
                nc.vector.tensor_scalar(x[:, :], x_scaled[:, :], gd_c[:, 0:1], bd_c[:, 0:1],
                                        ALU.mult, ALU.add).then_inc(x_ready, 1)

            def copy_sumx(b):
                dve.wait_ge(sumx_psum, b + 1)
                wait(dve, zk_psum, b)
                nc.vector.tensor_copy(zc[:, SIDE_END - 2:SIDE_END - 1], ps_sum).then_inc(sumx_ready, 1)

            def transpose_gram(b):
                dve.wait_ge(gram_ready, 4 * b + 4)
                wait(dve, zc_ready, b)
                nc.vector.transpose(zt[:, :], gram[:, 0:P, :].rearrange("p q g -> p (q g)")).then_inc(zt_ready, 1)
                wait(dve, zk_psum, b)
                nc.vector.transpose(zc[:, SIDE_AT:SIDE_AT + 2 * P],
                                    gram[:, P:TC, :].rearrange("p q g -> p (q g)"))
                dve.wait_ge(zt_ready, b + 1)
                for packed, piece in pair_pieces(zt, zc):
                    last = nc.vector.tensor_copy(packed, piece)
                last.then_inc(zc_ready, 1)

            def stats_z(b):
                dve.wait_ge(z_psum, b + 1)
                nc.vector.bn_stats(stats[:, :], ps_a[:, :]).then_inc(stats_ready, 1)
                dve.wait_ge(stats_ready, b + 1)
                dve.nop(nofuse=True)
                nc.vector.bn_aggr(mv[:, :], stats[:, :]).then_inc(mv_ready, 1)

            def shift_z(b):
                dve.wait_ge(zstd_ready, b + 1)
                wait(dve, z_ready, b)
                nc.vector.reciprocal(zrstd[:, :], zstd[:, :]).then_inc(zrstd_ready, 1)
                dve.wait_ge(zrstd_ready, b + 1)
                nc.vector.tensor_scalar(zshift[:, :], zrstd[:, :], mv[:, 0:1], -1.0, ALU.mult,
                                        ALU.mult).then_inc(zshift_ready, 1)

            done = [0]

            def link(instruction):
                done[0] += 1
                instruction.then_inc(prep_dve, 1)
                dve.wait_ge(prep_dve, done[0])

            nc.vector.memset(proj[:, :, :], 0.0)
            nc.vector.memset(gram_w[:, :], 0.0)
            nc.vector.memset(mean_ones[:, :], 1.0 / E)
            nc.vector.memset(ones[:, :], 1.0)
            nc.vector.memset(eps[:, :], EPS)
            nc.vector.memset(zc[:, SIDE_AT - 1:SIDE_AT], 0.0)
            nc.vector.memset(zc[:, SIDE_END - 1:SIDE_END], 1.0)
            nc.vector.memset(v[0][:, :, P + 1], 1.0)
            nc.vector.memset(v[1][:, :, P + 1], 1.0)
            link(nc.vector.memset(fold[:, :, :], 0.0))
            assert done[0] == DVE_CONST
            dve.wait_ge(interaction_w_in, 9 * DMA)
            link(nc.vector.tensor_reduce(wc_mean[:, :], wc[:, :], AX.X, ALU.add))
            link(nc.vector.tensor_scalar(wc_mean[:, :], wc_mean[:, :], 1.0 / E, None, ALU.mult))
            link(nc.vector.tensor_scalar(wc[:, :], wc[:, :], wc_mean[:, 0:1], None, ALU.subtract))
            assert done[0] == DVE_WC
            link(nc.vector.tensor_tensor(wcg[:, :], wc[:, :], gs_b[:, :], ALU.mult))
            dve.wait_ge(prep_pe, PE_GRAM)
            nc.vector.tensor_copy(gram_w[0:D, 0:D], ps_a[0:D, 0:D])
            link(nc.vector.tensor_copy(gram_w[D:2 * D, D:2 * D], ps_a[D:2 * D, D:2 * D]))
            assert done[0] == DVE_GRAM
            link(nc.vector.tensor_reduce(proj_mean[:, :], proj[:, :, :], AX.X, ALU.add))
            link(nc.vector.tensor_scalar(proj_mean[:, :], proj_mean[:, :], 1.0 / P, None, ALU.mult))
            link(nc.vector.tensor_tensor(proj[:, :, :], proj[:, :, :],
                                         proj_mean[:, :].unsqueeze(2).to_broadcast([ROWS, J, P]), ALU.subtract))
            assert done[0] == DVE_PROJ
            dve.wait_ge(x_w_in, 3 * DMA)
            link(nc.vector.tensor_reduce(wd_mean[:, :], wd[:, :, :], AX.X, ALU.add))
            link(nc.vector.scalar_tensor_tensor(
                wd[:, :, :], wd_mean[:, :].unsqueeze(2).to_broadcast([128, DK, E]), -1.0 / E, wd[:, :, :],
                ALU.mult, ALU.add))
            assert done[0] == DVE_WD
            quad_form(0, 0)
            sum_quad(0)
            scale_emb(0, 0, 0)
            quad_form(1, 1)
            sum_quad(1)
            dve.wait_ge(prep_pe, PE_YBIAS)
            link(nc.vector.tensor_copy(y_bias[:, :], ps_y[:, 0:P]))
            assert done[0] == DVE_YBIAS
            scale_x(0)
            finish_x(0)
            scale_emb(1, 1, 1)
            quad_form(2, 2)

            def fold_weights():
                dve.wait_ge(wl_in, 7 * DMA)
                a = coef[:, :, :]
                nc.vector.tensor_tensor(a[:, 0], bq[:, :], gp[:, :], ALU.mult)
                nc.vector.tensor_tensor(a[:, 1], bp[:, :], gq[:, :], ALU.mult)
                nc.vector.tensor_tensor(a[:, 2], gp[:, :], gq[:, :], ALU.mult)
                link(nc.vector.tensor_tensor(a[:, 3], bp[:, :], bq[:, :], ALU.mult))
                link(nc.vector.tensor_tensor(fold_q[:, :, :], isq[:, :, :],
                                             a[:, 1].unsqueeze(2).to_broadcast([128, KT, P]), ALU.mult))
                link(nc.vector.tensor_tensor(fold[:, :, P:2 * P], isp[:, :, :],
                                             a[:, 0].unsqueeze(2).to_broadcast([128, KT, P]), ALU.mult))
                link(nc.vector.tensor_tensor(fold[:, :, P:2 * P], fold[:, :, P:2 * P], fold_q[:, :, :], ALU.add))
                nc.vector.tensor_scalar(fold[:, :, SIDE - 1], a[:, 3], float(E), None, ALU.mult)
                nc.vector.tensor_copy(fold[0:P, KT - 1, SIDE - 2:SIDE - 1], bp[0:P, KT - 1:KT])
                link(nc.vector.tensor_scalar(fold[0:P, KT - 1, 0:P], ident[0:P, 0:P], gp[0:P, KT - 1:KT], None, ALU.mult))
                assert done[0] == DVE_FOLD
                dve.wait_ge(prep_pe, PE_FOLD)
                link(nc.vector.tensor_tensor(wl[:, :, :], wl[:, :, :],
                                             a[:, 2].unsqueeze(2).to_broadcast([128, KT, MAXD]), ALU.mult))
                assert done[0] == DVE_WL
                dve.wait_ge(prep_pe, PE_B1)
                link(nc.vector.tensor_tensor(b1_f[:, :], ps_b[:, 0:H1 // 128], b1_c[:, :], ALU.add))
                assert done[0] == DVE_B1
                for kt in range(ZK - 1):
                    nc.vector.tensor_scalar(w1_s[:, kt, :], w1_s[:, kt, :], gl_c[:, kt:kt + 1], None, ALU.mult)
                link(nc.vector.tensor_scalar(w1_s[:, ZK - 1, :], w1_s[:, ZK - 1, :], gl_c[:, ZK - 1:ZK], None, ALU.mult))
                assert done[0] == DVE_W1

            def body(b, first, last):
                b2 = not isinstance(b, int) or b >= 2
                for k in range(STEPS):
                    i = 4 * b + k
                    bias_y(i, 0)
                    bias_y(i, 1)
                    if not (last and k >= 2):
                        sum_quad(i + 2)
                    if k == 2:
                        copy_sumx(b)
                    sum_squares(i)
                    if not (last and k >= 2):
                        scale_emb(i + 2, (k + 2) % STEPS, k % 2)
                    if k == 2 and not first:
                        stats_z(b - 1)
                    normalise_y(i, b, k, k % 2)
                    if k == 0 and not last:
                        scale_x(b + 1)
                    if k == 2 and not first:
                        shift_z(b - 1)
                    if k == 3 and not last:
                        finish_x(b + 1)
                    if not (last and k >= 1):
                        quad_form(i + 3, (k + 3) % STEPS)
                    if k == 0 and not first:
                        transpose_gram(b - 1)
                if first:
                    fold_weights()

            blocks(dve, body)
            transpose_gram(NBLK - 1)
            stats_z(NBLK - 1)
            shift_z(NBLK - 1)

        @block.tensor
        def _(pe):
            mm = nc.tensor.matmul

            def transpose_emb(s, b, k):
                pe.wait_ge(gathered[k], GA * DMA * (b + 1))
                wait(pe, emb_t_ready, s)
                for t in range(PAIRS):
                    last = nc.tensor.transpose(ps_t[:, t * ROWS:(t + 1) * ROWS],
                                               emb[k][:, 2 * t:2 * t + 2, :].rearrange("r g d -> r (g d)"),
                                               ident[0:ROWS, 0:ROWS])
                last.then_inc(emb_t_psum, 1)

            def apply_gram_w(s, par):
                pe.wait_ge(emb_t_ready, s + 1)
                wait(pe, quad_ready, s)
                for t in range(PAIRS):
                    last = mm(ps_q[0:ROWS, t * 128:(t + 1) * 128], emb_t[par][:, t * ROWS:(t + 1) * ROWS], gram_w[:, :],
                              start=True, stop=True)
                last.then_inc(q_psum, 1)

            def project(s, par):
                pe.wait_ge(emb_r_ready, s + 1)
                wait(pe, mix_ready, s)
                for t in range(PAIRS):
                    last = mm(ps_m[:, t * 128:(t + 1) * 128],
                              emb_r[par][:, 2 * t:2 * t + 2, :].rearrange("r g d -> r (g d)"),
                              proj[:, :, :].rearrange("r j p -> r (j p)"), start=True, stop=True)
                last.then_inc(mix_psum, 1)

            def expand(s, par):
                pe.wait_ge(mix_ready, s + 1)
                for h in range(2):
                    wait(pe, y_ready, 2 * s - 1 + h)
                    mm(ps_y[:, h * 512:(h + 1) * 512], wcg[h * D:(h + 1) * D, :], mix[par][h * D:(h + 1) * D, :],
                       start=True, stop=True).then_inc(y_psum, 1)

            def gram_v(s, par):
                pe.wait_ge(v_ready, s + 1)
                wait(pe, gram_ready, s)
                for g in range(GA):
                    c = (g % 2) * (SPS // 2) + (g // 2) * J
                    for j in range(J):
                        last = mm(ps_z[32 * j:32 * j + 32, g * TC:(g + 1) * TC], v[par][:, c + j, 0:P],
                                  v[par][:, c + j, :], start=True, stop=True)
                last.then_inc(gram_psum, 1)

            def project_x(b):
                pe.wait_ge(dense_x_in, DMA * (b + 1))
                wait(pe, x_scaled_ready, b)
                wait(pe, z_t_ready, b - 2)
                for kt in range(DK):
                    last = mm(ps_x, wd[:, kt, :], dense_x[:, kt, :], start=(kt == 0), stop=(kt == DK - 1))
                last.then_inc(x_psum, 1)

            def variance_x(b):
                pe.wait_ge(xsq_ready, b + 1)
                mm(ps_xv, mean_ones[:, :], xsq[:, :], start=True, stop=True).then_inc(xvar_psum, 1)

            def sum_x(b):
                pe.wait_ge(x_ready, b + 1)
                mm(ps_sum, x[:, :], ones[:, :], start=True, stop=True).then_inc(sumx_psum, 1)

            def transpose_z_pairs(b, x_blocks):
                pe.wait_ge(zc_ready, b + 1)
                pe.wait_ge(x_scaled_ready, x_blocks)
                wait(pe, score_ready, b)
                for t in range(KT - 1):
                    nc.tensor.transpose(ps_a[:, t * BLK:(t + 1) * BLK], zc[:, t * 128:(t + 1) * 128], ident[:, :])
                nc.tensor.transpose(ps_b[0:KL, 0:BLK], zc[:, 128 * (KT - 1):ZROWS], ident[:, :]).then_inc(zk_psum, 1)

            def z_first(b):
                pe.wait_ge(zk_ready, b + 1)
                for t in range(3):
                    mm(ps_a[:, :], zk[:, t, :], wl[:, t, :], start=(t == 0), stop=False)

            def z_second(b):
                for t in range(3, KT):
                    rows = 128 if t < KT - 1 else KL
                    last = mm(ps_a[:, :], zk[0:rows, t, :], wl[0:rows, t, :], start=False, stop=(t == KT - 1))
                last.then_inc(z_psum, 1)

            def transpose_z(b, x_blocks):
                pe.wait_ge(z_ready, b + 1)
                pe.wait_ge(sumx_ready, x_blocks)
                for t in range(ZK):
                    last = nc.tensor.transpose(ps_b[:, t * BLK:(t + 1) * BLK], z[:, t * 128:(t + 1) * 128], ident[:, :])
                last.then_inc(z_t_psum, 1)

            def top1(b, half):
                if half == 0:
                    pe.wait_ge(z_t_ready, b + 1)
                    pe.wait_ge(dense_h_in, DMA * (b + 1))
                for m in range(half * 2, half * 2 + 2):
                    for kt in range(ZK + DK):
                        rhs = z_t[:, kt, :] if kt < ZK else dense_h[:, kt - ZK, :]
                        last = mm(ps_a[:, m * BLK:(m + 1) * BLK], w1_s[:, kt, m * 128:(m + 1) * 128], rhs,
                                  start=(kt == 0), stop=(kt == ZK + DK - 1))
                if half == 1:
                    last.then_inc(h1_psum, 1)

            def top2(b):
                pe.wait_ge(h1_ready, b + 1)
                n = H1 // 128
                for m in range(H2 // 128):
                    for kt in range(n):
                        last = mm(ps_a[:, m * BLK:(m + 1) * BLK], w2_s[:, kt, m * 128:(m + 1) * 128], h1[:, kt, :],
                                  start=(kt == 0), stop=(kt == n - 1))
                last.then_inc(h2_psum, 1)

            def top3(b):
                pe.wait_ge(h2_ready, b + 1)
                n = H2 // 128
                for kt in range(n):
                    last = mm(ps_a[0:1, 256:384], w3_s[:, kt:kt + 1], h2[:, kt, :], start=(kt == 0), stop=(kt == n - 1))
                last.then_inc(score_psum, 1)

            pe.wait_ge(prep_dve, DVE_WC)
            nc.tensor.transpose(ps_a[:, 0:2 * D], wc[:, :], ident[:, :]).then_inc(prep_pe, 1)
            pe.wait_ge(prep_act, ACT_WCE)
            mm(ps_a[:, 0:2 * D], wc_e[:, :], wc_e[:, :], start=True, stop=True).then_inc(prep_pe, 1)
            pe.wait_ge(prep_dve, DVE_PROJ)
            mm(ps_y[:, 0:P], bs_b[:, :], proj[0:NF, 0, :], start=True, stop=True).then_inc(prep_pe, 1)
            pe.wait_ge(prep_dve, DVE_WD)
            project_x(0)
            transpose_emb(0, 0, 0)
            apply_gram_w(0, 0)
            transpose_emb(1, 0, 1)
            variance_x(0)
            apply_gram_w(1, 1)
            project(0, 0)
            transpose_emb(2, 0, 2)
            apply_gram_w(2, 0)
            pe.wait_ge(prep_dve, DVE_YBIAS)

            def body(b, first, last):
                b2 = not isinstance(b, int) or b >= 2
                for k in range(STEPS):
                    i = 4 * b + k
                    expand(i, k % 2)
                    if k == 0:
                        if b2:
                            top2(b - 2)
                        if not last:
                            project_x(b + 1)
                    if k == 2 and not first:
                        z_second(b - 1)
                    if k == 3 and not first:
                        transpose_z(b - 1, b + 1)
                    if not (last and k >= 1):
                        transpose_emb(i + 3, b + (k + 3) // STEPS, (k + 3) % STEPS)
                    if not (last and k == 3):
                        project(i + 1, (k + 1) % 2)
                    if k == 0:
                        if b2:
                            top3(b - 2)
                        if not last:
                            variance_x(b + 1)
                    if k == 1 and not first:
                        transpose_z_pairs(b - 1, NBLK if last else b + 2)
                    if k == 3 and not first:
                        top1(b - 1, 0)
                    if not (first and k == 0):
                        gram_v(i - 1, (k + 1) % 2)
                    if not (last and k >= 1):
                        apply_gram_w(i + 3, (k + 1) % 2)
                    if k == 1:
                        if not first:
                            z_first(b - 1)
                        sum_x(b)
                    if k == 3 and not first:
                        top1(b - 1, 1)
                if first:
                    pe.wait_ge(prep_dve, DVE_FOLD)
                    for t in range(KT):
                        last = mm(ps_a[0:SIDE, :], fold[:, t, :], wl[:, t, :], start=(t == 0), stop=(t == KT - 1))
                    last.then_inc(prep_pe, 1)
                    pe.wait_ge(sumx_ready, 1)
                    pe.wait_ge(x_scaled_ready, 2)
                    pe.wait_ge(mlp_w_in, 7 * DMA)
                    for m in range(H1 // 128):
                        for kt in range(ZK):
                            last = mm(ps_b[:, m:m + 1], w1_s[:, kt, m * 128:(m + 1) * 128], bl_c[:, kt:kt + 1],
                                      start=(kt == 0), stop=(kt == ZK - 1))
                    last.then_inc(prep_pe, 1)
                    pe.wait_ge(prep_dve, DVE_W1)
                    pe.wait_ge(prep_act, ACT_FOLD)

            blocks(pe, body)
            b = NBLK - 1
            gram_v(NS - 1, (NS - 1) % 2)
            top2(b - 1)
            top3(b - 1)
            transpose_z_pairs(b, NBLK)
            z_first(b)
            z_second(b)
            transpose_z(b, NBLK)
            top1(b, 0)
            top1(b, 1)
            top2(b)
            top3(b)


def kernel(**inputs):
    import numpy as np
    import concourse.bacc as bacc
    from concourse.bass_utils import run_bass_kernel_spmd

    def f(name):
        return np.asarray(inputs[name])

    tables = [f(f"tbl_{n}") for n in range(NF)]
    base = np.cumsum([0] + [t.shape[0] for t in tables[:-1]]).astype(np.int32)
    wl = f("L0_rec_Wl")
    gsi, bsi = f("L0_rec_gsi"), f("L0_rec_bsi")
    wl_pairs = np.zeros((128, KT, MAXD), wl.dtype)
    of_p = np.zeros((128, KT), np.int64)
    of_q = np.zeros((128, KT), np.int64)
    is_p = np.zeros((128, KT, P), np.float32)
    is_q = np.zeros((128, KT, P), np.float32)
    b_of_p, b_of_q = np.zeros((2, 128, KT), bsi.dtype)
    rows_of_wl = set()
    for row, q, p in pair_order():
        r, t = row % 128, row // 128
        of_p[r, t], of_q[r, t] = p, q
        b_of_p[r, t], b_of_q[r, t] = bsi[p], bsi[q]
        is_p[r, t, p] = is_q[r, t, q] = 1.0
        if p > q and (q, p) not in rows_of_wl:
            rows_of_wl.add((q, p))
            wl_pairs[r, t] = wl[:, (p + 1) * p // 2 + q + 1]
    assert len(rows_of_wl) == P * (P - 1) // 2
    for p in range(P):
        of_p[p, KT - 1] = p
        b_of_p[p, KT - 1] = bsi[p]
        wl_pairs[p, KT - 1] = wl[:, (p + 1) * p // 2]

    def columns(a):
        return np.ascontiguousarray(a.reshape(-1, 128).T)

    def k_tiles(a):
        return np.ascontiguousarray(a.reshape(-1, 128, a.shape[1]).transpose(1, 0, 2))

    w1 = f("W_top1")
    arrays = {
        "dense_t": k_tiles(f("r_dense_t").T),
        "ids": np.ascontiguousarray(f("ids").reshape(NBLK, J, STEPS * GA, NF).transpose(1, 3, 0, 2).reshape(ROWS, -1)),
        "row_base": np.tile(base, J).reshape(ROWS, 1),
        "tables": np.concatenate(tables, axis=0),
        "ws_t": np.ascontiguousarray(f("L0_rec_Ws").T),
        "gs": f("L0_rec_gs"),
        "bs": f("L0_rec_bs"),
        "wsi_t": np.ascontiguousarray(f("L0_rec_Wsi").T),
        "wd_t": k_tiles(f("L0_rec_Wd").T),
        "gd": columns(f("L0_rec_gd")),
        "bd": columns(f("L0_rec_bd")),
        "wl_pairs": wl_pairs,
        "g_of_p": gsi[of_p],
        "g_of_q": gsi[of_q],
        "b_of_p": b_of_p,
        "b_of_q": b_of_q,
        "is_p": is_p,
        "is_q": is_q,
        "identity": np.eye(128, dtype=np.float32),
        "gl": columns(f("L0_rec_gl")[:DIMS]),
        "bl": columns(f("L0_rec_bl")[:DIMS]),
        "w1": k_tiles(np.concatenate([w1[:DIMS], w1[MAXD:]], axis=0)),
        "b1": columns(f("b_top1")),
        "w2": k_tiles(f("W_top2")),
        "b2": columns(f("b_top2")),
        "w3": columns(f("W_top3").reshape(-1)),
    }
    nc = bacc.Bacc("TRN2", target_bir_lowering=False, num_devices=1)
    args = [nc.dram_tensor(f"in_{name}", a.shape, mybir.dt.from_np(a.dtype), kind="ExternalInput").ap()
            for name, a in arrays.items()]
    out = nc.dram_tensor("scores", (1, B), F32, kind="ExternalOutput").ap()
    dlrm_kernel(nc, *args, out)
    r = run_bass_kernel_spmd(nc, [{f"in_{name}": a for name, a in arrays.items()}], core_ids=[0])
    return r.results[0]["scores"].reshape(B, 1)
```

```python
import concourse.bass as bass
from concourse import mybir
from contextlib import ExitStack

F32 = mybir.dt.float32
I32 = mybir.dt.int32
ALU = mybir.AluOpType
ACT = mybir.ActivationFunctionType
AX = mybir.AxisListType

B, DENSE, NF, D, E, P = 2048, 256, 26, 64, 128, 32
MAXD, DIMS = 512, 384
H1, H2 = 512, 256
EPS = 1e-5
BLK = 128
NBLK = B // BLK
STEPS = 4
ROWS = 128
FULL = 4
HEAD = ROWS - FULL * NF
REST = NF - HEAD
REG = 6
UNITS = REG // 2
COLS = 1 + UNITS * (FULL + 1)
SPS = 2 * COLS
GATHERS = [REG + 2] + [REG] * (STEPS - 1)
BGA = sum(GATHERS)
GA = max(GATHERS)
SQ = 4
TC = P + 2
NS = NBLK * STEPS
SIDE = 2 * P + 2
SIDE_AT = 512
SIDE_END = SIDE_AT + SIDE
ZROWS = SIDE_END + 9
KT = 5
KL = ZROWS - 128 * (KT - 1)
ZK = DIMS // 128
DK = DENSE // 128
DMA = 16


def pair_order():
    order = [(q, q + 1 + c) for q in range(16) for c in range(16)]
    order += [(16 * t + q, 17 + q + c) for t in range(2) for q in range(8) for c in range(8)]
    order += [(8 * t + q, 25 + q + c) for t in range(4) for q in range(4) for c in range(4)]
    order += [(4 * t + q, 29 + c) for t in range(8) for q in range(3) for c in range(3)]
    return [(r if r < 511 else r - 511 + SIDE_END, q, p) for r, (q, p) in enumerate(order)]


def pair_pieces(zt, packed):
    def bands(triangles, start, rows, width):
        part = zt[:, 0:P * P].rearrange("s (t m) -> s t m", t=triangles)[:, :, start:start + rows * (P + 1)]
        return part.rearrange("s t (q c) -> s t q c", c=P + 1)[:, :, :, 0:width]

    def at(first, last, triangles, width):
        return packed[:, first:last].rearrange("s (t q c) -> s t q c", t=triangles, c=width)

    corners = zt[:, 0:P * P].rearrange("s (t q p) -> s t q p", t=8, p=P)[:, :, 0:3, P - 3:P]
    return [(at(0, 256, 1, 16)[:, 0], bands(1, 1, 16, 16)[:, 0]),
            (at(256, 384, 2, 8), bands(2, 17, 8, 8)),
            (at(384, 448, 4, 4), bands(4, 25, 4, 4)),
            (at(448, 511, 7, 3), corners[:, 0:7]),
            (at(SIDE_END, SIDE_END + 9, 1, 3)[:, 0], corners[:, 7])]


def dlrm_kernel(nc, dense_t, ids, row_base, tables, ws_t, gs, bs, wsi_t, wd_t, gd, bd, wl_pairs,
                g_of_p, g_of_q, b_of_p, b_of_q, is_p, is_q, identity, gl, bl, w1, b1, w2, b2, w3, out):
    ctx = ExitStack()

    def sb(name, shape, dt=F32):
        return ctx.enter_context(nc.sbuf_tensor(name, shape, dt))

    def pb(name, shape):
        return ctx.enter_context(nc.psum_tensor(name, shape, F32))

    def sem(name):
        return ctx.enter_context(nc.semaphore(name))

    with ctx:
        ident = sb("ident", [128, 128])
        feature_id = sb("feature_id", [ROWS, NBLK * BGA], I32)
        rows = [sb(f"rows{k}", [ROWS, GATHERS[k]], I32) for k in range(STEPS)]
        base = sb("base", [ROWS, GA], I32)
        wc = sb("wc", [2 * D, E])
        wcg = sb("wcg", [2 * D, E])
        wc_e = sb("wc_e", [E, 2 * D])
        gram_w = sb("gram_w", [2 * D, 2 * D])
        NPROJ = FULL + 1 + STEPS * (1 + UNITS)
        proj = sb("proj", [ROWS, NPROJ, P])
        proj_mean = sb("proj_mean", [ROWS, NPROJ])
        gs_b = sb("gs_b", [2 * D, E])
        bs_b = sb("bs_b", [NF, E])
        y_bias = sb("y_bias", [E, P])
        wd = sb("wd", [128, DK, E])
        wd_mean = sb("wd_mean", [128, DK])
        wc_mean = sb("wc_mean", [2 * D, 1])
        gd_c = sb("gd_c", [E, 1])
        bd_c = sb("bd_c", [E, 1])
        ones = sb("ones", [E, 1])
        table_warm = sb("table_warm", [128, 1])
        wl = sb("wl", [128, KT, MAXD])
        gp = sb("gp", [128, KT])
        gq = sb("gq", [128, KT])
        bp = sb("bp", [128, KT])
        bq = sb("bq", [128, KT])
        isp = sb("isp", [128, KT, P])
        isq = sb("isq", [128, KT, P])
        coef = sb("coef", [128, 4, KT])
        fold = sb("fold", [128, KT, SIDE])
        fold_q = sb("fold_q", [128, KT, P])
        w1_s = sb("w1_s", [128, ZK + DK, H1])
        gl_c = sb("gl_c", [128, ZK])
        bl_c = sb("bl_c", [128, ZK])
        b1_c = sb("b1_c", [128, H1 // 128])
        w2_s = sb("w2_s", [128, H1 // 128, H2])
        b2_c = sb("b2_c", [128, H2 // 128])
        w3_s = sb("w3_s", [128, H2 // 128])
        emb = [sb(f"emb{k}", [ROWS, GATHERS[k], D]) for k in range(STEPS)]
        emb_t = [sb(f"emb_t{i}", [2 * D, GA // 2 * ROWS]) for i in range(2)]
        quad = sb("quad", [ROWS, GA, D])
        var = sb("var", [ROWS, GA])
        eps = sb("eps", [128, 1])
        std = sb("std", [ROWS, GA])
        rstd = sb("rstd", [ROWS, GA])
        emb_r = [sb(f"emb_r{i}", [ROWS, REG, D]) for i in range(2)]
        emb_s = sb("emb_s", [ROWS, 2, D])
        mix = [sb(f"mix{i}", [2 * D, COLS * P]) for i in range(2)]
        y = sb("y", [E, SPS, P])
        ysq = sb("ysq", [E, SPS, P])
        yvar = sb("yvar", [E, SPS])
        ystd = sb("ystd", [E, SPS])
        yrstd = sb("yrstd", [E, SPS])
        v = [sb(f"v{i}", [E, SPS, TC]) for i in range(2)]
        dense_x = sb("dense_x", [128, DK, BLK])
        dense_h = sb("dense_h", [128, DK, BLK])
        xsq = sb("xsq", [BLK, E])
        xvar = sb("xvar", [BLK, 1])
        xstd = sb("xstd", [BLK, 1])
        xrstd = sb("xrstd", [BLK, 1])
        x_scaled = sb("x_scaled", [BLK, E])
        x_next = sb("x_next", [E, BLK])
        x = sb("x", [E, BLK])
        gram = sb("gram", [128, TC, BLK // SQ])
        zt = sb("zt", [BLK, P * P])
        zc = sb("zc", [BLK, ZROWS])
        zk = sb("zk", [128, KT, BLK])
        stats = sb("stats", [BLK, 6])
        mv = sb("mv", [BLK, 2])
        zstd = sb("zstd", [BLK, 1])
        zrstd = sb("zrstd", [BLK, 1])
        zshift = sb("zshift", [BLK, 1])
        z = sb("z", [BLK, DIMS])
        z_t = sb("z_t", [128, ZK, BLK])
        h1 = sb("h1", [128, H1 // 128, BLK])
        h2 = sb("h2", [128, H2 // 128, BLK])
        scores = sb("scores_sb", [BLK, NBLK])
        ps_t = pb("ps_t", [128, 512])
        ps_q = pb("ps_q", [128, 512])
        ps_m = pb("ps_m", [128, 512])
        ps_y = pb("ps_y", [128, 1024])
        ps_z = pb("ps_z", [128, 512])
        ps_a = pb("ps_a", [128, 512])
        ps_b = pb("ps_b", [128, 512])
        ps_sum = ps_b[:, 0:1]
        ps_x = ps_b[:, 384:512]
        ps_xt = ps_b[:, 256:384]

        ids_in = sem("ids_in")
        ws_in = sem("ws_in")
        interaction_w_in = sem("interaction_w_in")
        x_w_in = sem("x_w_in")
        fold_in = sem("fold_in")
        wl_in = sem("wl_in")
        mlp_w_in = sem("mlp_w_in")
        dense_x_in = sem("dense_x_in")
        dense_h_in = sem("dense_h_in")
        gathered = [sem(f"gathered{k}") for k in range(STEPS)]
        out_done = sem("out_done")
        prep_dve = sem("prep_dve")
        prep_pe = sem("prep_pe")
        prep_act = sem("prep_act")
        rows_ready = sem("rows_ready")
        emb_t_psum = sem("emb_t_psum")
        emb_t_ready = sem("emb_t_ready")
        q_psum = sem("q_psum")
        quad_ready = sem("quad_ready")
        var_ready = sem("var_ready")
        std_ready = sem("std_ready")
        rstd_ready = sem("rstd_ready")
        emb_r_ready = sem("emb_r_ready")
        special_ready = sem("special_ready")
        mix_psum = sem("mix_psum")
        mix_ready = sem("mix_ready")
        y_psum = sem("y_psum")
        y_ready = sem("y_ready")
        ysq_ready = sem("ysq_ready")
        yvar_ready = sem("yvar_ready")
        ystd_ready = sem("ystd_ready")
        yrstd_ready = sem("yrstd_ready")
        v_ready = sem("v_ready")
        gram_psum = sem("gram_psum")
        gram_ready = sem("gram_ready")
        x_psum = sem("x_psum")
        xsq_ready = sem("xsq_ready")
        xstd_ready = sem("xstd_ready")
        xrstd_ready = sem("xrstd_ready")
        x_scaled_ready = sem("x_scaled_ready")
        xt_psum = sem("xt_psum")
        x_next_ready = sem("x_next_ready")
        x_ready = sem("x_ready")
        sumx_psum = sem("sumx_psum")
        sumx_ready = sem("sumx_ready")
        zt_ready = sem("zt_ready")
        zc_ready = sem("zc_ready")
        zk_psum = sem("zk_psum")
        zk_ready = sem("zk_ready")
        z_psum = sem("z_psum")
        stats_ready = sem("stats_ready")
        mv_ready = sem("mv_ready")
        zstd_ready = sem("zstd_ready")
        zrstd_ready = sem("zrstd_ready")
        zshift_ready = sem("zshift_ready")
        z_ready = sem("z_ready")
        z_t_psum = sem("z_t_psum")
        z_t_ready = sem("z_t_ready")
        h1_psum = sem("h1_psum")
        h1_ready = sem("h1_ready")
        h2_psum = sem("h2_psum")
        h2_ready = sem("h2_ready")
        score_psum = sem("score_psum")
        score_ready = sem("score_ready")

        FOLD_LOADS, MLP_LOADS = 6, 6 + ZK + DK
        DVE_CONST, DVE_WC, DVE_GRAM, DVE_PROJ, DVE_WD, DVE_FOLD, DVE_YBIAS = 1, 4, 6, 9, 11, 16, 17
        PE_WCE, PE_GRAM, PE_YBIAS, PE_FOLD = 1, 2, 3, 4
        ACT_WCE, ACT_WL, ACT_FOLD = 1, 2, 3

        def wait(engine, semaphore, count):
            if not isinstance(count, int) or count > 0:
                engine.wait_ge(semaphore, count)

        def blocks(engine, body):
            body(0, True, False)
            body(1, False, False)
            with engine.Fori(2, NBLK - 1) as b:
                body(b, False, False)
            body(NBLK - 1, False, True)

        block = ctx.enter_context(nc.Block())

        @block.sync
        def _(sp):
            sp.dma_start(feature_id[:, :], ids).then_inc(ids_in, DMA)
            sp.dma_start(base[:, :], row_base).then_inc(ids_in, DMA)
            sp.dma_start(proj[:, :, :], wsi_t).then_inc(interaction_w_in, DMA)
            sp.dma_start(bs_b[:, :], bs.partition_broadcast(NF)).then_inc(interaction_w_in, DMA)
            sp.dma_start(dense_x[:, :, :], dense_t[:, :, 0:BLK]).then_inc(dense_x_in, DMA)
            sp.dma_start(gd_c[:, :], gd).then_inc(x_w_in, DMA)
            sp.dma_start(bd_c[:, :], bd).then_inc(x_w_in, DMA)
            for tile, source in ((gp, g_of_p), (gq, g_of_q), (bp, b_of_p), (bq, b_of_q)):
                sp.dma_start(tile[:, :], source).then_inc(fold_in, DMA)
            sp.dma_start(isp[:, :, :], is_p).then_inc(fold_in, DMA)
            sp.dma_start(isq[:, :, :], is_q).then_inc(fold_in, DMA)

            def later_weights():
                sp.wait_ge(gathered[0], GATHERS[0] * DMA)
                for t in range(KT):
                    sp.dma_start(wl[:, t, :], wl_pairs[:, t, :]).then_inc(wl_in, DMA)
                sp.wait_ge(gathered[3], GATHERS[3] * DMA)
                for t in range(ZK + DK):
                    sp.dma_start(w1_s[:, t, :], w1[:, t, :]).then_inc(mlp_w_in, DMA)
                for tile, source in ((w3_s, w3), (gl_c, gl), (bl_c, bl), (b1_c, b1), (b2_c, b2)):
                    sp.dma_start(tile[:, :], source).then_inc(mlp_w_in, DMA)
                sp.dma_start(w2_s[:, :, :], w2).then_inc(mlp_w_in, DMA)

            def dense_for_x(b):
                sp.wait_ge(x_psum, b)
                sp.dma_start(dense_x[:, :, :], dense_t[:, :, bass.ds(b * BLK, BLK)]).then_inc(dense_x_in, DMA)

            def body(b, first, last):
                if first:
                    dense_for_x(1)
                    later_weights()
                if not last:
                    dense_for_x(b + 2)
                wait(sp, h1_psum, b)
                sp.dma_start(dense_h[:, :, :], dense_t[:, :, bass.ds(b * BLK, BLK)]).then_inc(dense_h_in, DMA)

            body(0, True, False)
            with sp.Fori(1, NBLK - 2) as b:
                body(b, False, False)
            body(NBLK - 2, False, True)
            body(NBLK - 1, False, True)
            sp.wait_ge(score_ready, NBLK)
            sp.dma_start(out, scores[:, :]).then_inc(out_done, DMA)
            sp.wait_ge(out_done, DMA)

        @block.gpsimd
        def _(pool):
            pool.wait_ge(ids_in, 2 * DMA)

            def body(b, first, last):
                for k in range(STEPS):
                    n, at = GATHERS[k], sum(GATHERS[:k])
                    if not first:
                        pool.wait_ge(gathered[k], n * DMA * b)
                    pool.tensor_tensor(rows[k][:, :], feature_id[:, bass.ds(b * BGA + at, n)],
                                       base[:, 0:n], ALU.add).then_inc(rows_ready, 1)
                    if not first and k == 0:
                        pool.wait_ge(special_ready, b)
                    elif not first:
                        pool.wait_ge(emb_r_ready, 4 * b - 3 + k)
                    pool.wait_ge(rows_ready, 4 * b + k + 1)
                    pool.nop(nofuse=True)
                    for g in range(n):
                        pool.indirect_dma_start(
                            out=emb[k][:, g, :], out_offset=None, in_=tables,
                            in_offset=bass.IndirectOffsetOnAxis(ap=rows[k][:, g:g + 1], axis=0),
                        ).then_inc(gathered[k], DMA)

            blocks(pool, body)

        @block.scalar
        def _(act):
            act.dma_start(wc[0:D, :], ws_t).then_inc(ws_in, DMA)
            act.dma_start(wc[D:2 * D, :], ws_t).then_inc(ws_in, DMA)
            act.dma_start(ident[:, :], identity).then_inc(ws_in, DMA)
            act.dma_start(gs_b[:, :], gs.partition_broadcast(2 * D)).then_inc(ws_in, DMA)
            act.dma_start(wd[:, :, :], wd_t).then_inc(x_w_in, DMA)
            act.wait_ge(prep_dve, DVE_CONST)
            nc.scalar.activation(table_warm[:, :], eps[:, 0:1], ACT.Sqrt)

            def copy_emb_t(s, k, par):
                act.wait_ge(emb_t_psum, s + 1)
                wait(act, q_psum, s - 1)
                n = GATHERS[k] // 2 * ROWS
                nc.scalar.copy(emb_t[par][:, 0:n], ps_t[:, 0:n]).then_inc(emb_t_ready, 1)

            def copy_mix(s, par):
                act.wait_ge(mix_psum, s + 1)
                wait(act, y_psum, 2 * s - 2)
                nc.scalar.copy(mix[par][:, :], ps_m[:, :]).then_inc(mix_ready, 1)

            def std_emb(s, k):
                act.wait_ge(var_ready, s + 1)
                wait(act, rstd_ready, s)
                n = GATHERS[k]
                nc.scalar.activation(std[:, 0:n], var[:, 0:n], ACT.Sqrt, bias=eps[:, 0:1],
                                     scale=1.0 / E).then_inc(std_ready, 1)

            def std_y(s):
                act.wait_ge(yvar_ready, s + 1)
                wait(act, yrstd_ready, s)
                nc.scalar.activation(ystd[:, :], yvar[:, :], ACT.Sqrt, bias=eps[:, 0:1],
                                     scale=1.0 / P).then_inc(ystd_ready, 1)

            def std_x(b):
                act.wait_ge(xsq_ready, b + 1)
                wait(act, xrstd_ready, b)
                nc.scalar.activation(xstd[:, :], xvar[:, :], ACT.Sqrt, bias=eps[:, 0:1],
                                     scale=1.0 / E).then_inc(xstd_ready, 1)

            def gain_x(b):
                act.wait_ge(xt_psum, b + 1)
                act.wait_ge(x_w_in, 3 * DMA)
                wait(act, x_ready, b)
                nc.scalar.activation(x_next[:, :], ps_xt, ACT.Identity, bias=bd_c[:, 0:1],
                                     scale=gd_c[:, 0:1]).then_inc(x_next_ready, 1)

            def std_z(b):
                act.wait_ge(mv_ready, b + 1)
                wait(act, zrstd_ready, b)
                nc.scalar.activation(zstd[:, :], mv[:, 1:2], ACT.Sqrt, bias=eps[:, 0:1]).then_inc(zstd_ready, 1)

            def square_y(s, h):
                act.wait_ge(y_ready, 2 * s + 1 + h)
                if h == 0:
                    wait(act, yvar_ready, s)
                c = slice(h * SPS // 2, (h + 1) * SPS // 2)
                nc.scalar.activation(ysq[:, c, :], y[:, c, :], ACT.Square).then_inc(ysq_ready, 1)

            def copy_gram(s, b, k):
                act.wait_ge(gram_psum, s + 1)
                if k == 0:
                    wait(act, zc_ready, b)
                src = ps_z[:, 0:SPS // SQ * TC].rearrange("p (g q) -> p q g", q=TC)
                nc.scalar.copy(gram[:, :, k * (SPS // SQ):(k + 1) * (SPS // SQ)], src).then_inc(gram_ready, 1)

            def square_x(b):
                act.wait_ge(x_psum, b + 1)
                wait(act, xstd_ready, b)
                nc.scalar.activation(xsq[:, :], ps_x, ACT.Square, accum_out=xvar[:, :]).then_inc(xsq_ready, 1)

            def copy_zk(b):
                act.wait_ge(zk_psum, b + 1)
                wait(act, z_psum, b)
                nc.scalar.copy(zk[:, 0:4, :], ps_a[:, :].rearrange("p (t s) -> p t s", t=4))
                nc.scalar.copy(zk[0:KL, KT - 1, :], ps_b[0:KL, 0:BLK]).then_inc(zk_ready, 1)

            def normalise_z(b):
                act.wait_ge(zshift_ready, b + 1)
                wait(act, z_t_psum, b)
                nc.scalar.activation(z[:, :], ps_a[:, 0:DIMS], ACT.Identity, bias=zshift[:, 0:1],
                                     scale=zrstd[:, 0:1]).then_inc(z_ready, 1)

            def gain_z(b):
                act.wait_ge(z_t_psum, b + 1)
                if isinstance(b, int) and b == 0:
                    act.wait_ge(mlp_w_in, MLP_LOADS * DMA)
                wait(act, h1_psum, b)
                for t in range(ZK):
                    last = nc.scalar.activation(z_t[:, t, :], ps_b[:, t * BLK:(t + 1) * BLK], ACT.Identity,
                                                bias=bl_c[:, t:t + 1], scale=gl_c[:, t:t + 1])
                last.then_inc(z_t_ready, 1)

            def relu_h1(b, ps):
                act.wait_ge(h1_psum, b + 1)
                wait(act, h2_psum, b)
                for m in range(H1 // 128):
                    last = nc.scalar.activation(h1[:, m, :], ps[:, m * BLK:(m + 1) * BLK], ACT.Relu,
                                                bias=b1_c[:, m:m + 1])
                last.then_inc(h1_ready, 1)

            def relu_h2(b, ps):
                act.wait_ge(h2_psum, b + 1)
                wait(act, score_psum, b)
                for m in range(H2 // 128):
                    last = nc.scalar.activation(h2[:, m, :], ps[:, m * BLK:(m + 1) * BLK], ACT.Relu,
                                                bias=b2_c[:, m:m + 1])
                last.then_inc(h2_ready, 1)

            def copy_score(b, ps):
                act.wait_ge(score_psum, b + 1)
                nc.scalar.copy(scores[:, bass.ds(b, 1)], ps[:, H2:H2 + 1]).then_inc(score_ready, 1)

            def scale_wl(first_tile, end):
                act.wait_ge(prep_pe, PE_FOLD)
                act.wait_ge(prep_dve, DVE_FOLD)
                for t in range(first_tile, end):
                    last = nc.scalar.activation(wl[:, t, :], wl[:, t, :], ACT.Identity, scale=coef[:, 2, t:t + 1])
                if end == KT:
                    last.then_inc(prep_act, 1)

            act.wait_ge(prep_pe, PE_WCE)
            nc.scalar.copy(wc_e[:, :], ps_a[:, 0:2 * D]).then_inc(prep_act, 1)
            copy_emb_t(0, 0, 0)
            square_x(0)
            copy_emb_t(1, 1, 1)
            std_emb(0, 0)
            std_x(0)
            gain_x(0)
            copy_mix(0, 0)
            copy_emb_t(2, 2, 0)
            std_emb(1, 1)

            def first_block():
                for i in range(STEPS):
                    if i == 1:
                        gain_x(1)
                    square_y(i, 0)
                    square_y(i, 1)
                    copy_mix(i + 1, (i + 1) % 2)
                    std_emb(i + 2, (i + 2) % STEPS)
                    if i == 0:
                        square_x(1)
                    std_y(i)
                    if i == 0:
                        std_x(1)
                    else:
                        copy_gram(i - 1, 0, i - 1)
                    copy_emb_t(i + 3, (i + 3) % STEPS, (i + 1) % 2)
                    if i == 2:
                        scale_wl(0, 3)
                scale_wl(3, KT)
                act.wait_ge(prep_act, ACT_WL)
                nc.scalar.copy(wl[0:SIDE, KT - 1, :], ps_a[0:SIDE, :]).then_inc(prep_act, 1)

            def body(b, first, last):
                if first:
                    first_block()
                    return
                b2 = not isinstance(b, int) or b >= 2
                for k in range(STEPS):
                    i = 4 * b + k
                    newest_last = not b2 and k < 2
                    if k == 0 and b2:
                        relu_h1(b - 2, ps_a)
                    if k == 1 and not last:
                        gain_x(b + 1)
                    if k % 2 == 1 and not last and not newest_last:
                        copy_emb_t(i + 3, (k + 3) % STEPS, (k + 1) % 2)
                    square_y(i, 0)
                    square_y(i, 1)
                    if k == 1:
                        copy_mix(i + 1, (k + 1) % 2)
                        copy_zk(b - 1)
                    if not (last and k >= 2):
                        std_emb(i + 2, (k + 2) % STEPS)
                    if k == 0:
                        if b2:
                            relu_h2(b - 2, ps_a)
                        if not last:
                            square_x(b + 1)
                    if k % 2 == 0 and not (last and k >= 1) and not newest_last:
                        copy_emb_t(i + 3, (k + 3) % STEPS, (k + 1) % 2)
                    if k == 3:
                        gain_z(b - 1)
                    std_y(i)
                    if k != 1 and not (last and k == 3):
                        copy_mix(i + 1, (k + 1) % 2)
                    if k == 0:
                        if b2:
                            copy_score(b - 2, ps_a)
                        if not last:
                            std_x(b + 1)
                    if k == 2:
                        std_z(b - 1)
                    if k > 0:
                        copy_gram(i - 1, b, k - 1)
                    else:
                        copy_gram(i - 1, b - 1, STEPS - 1)
                    if k == 2:
                        normalise_z(b - 1)
                    if newest_last:
                        copy_emb_t(i + 3, (k + 3) % STEPS, (k + 1) % 2)

            blocks(act, body)
            b = NBLK - 1
            relu_h1(b - 1, ps_a)
            copy_gram(NS - 1, b, STEPS - 1)
            relu_h2(b - 1, ps_m)
            copy_zk(b)
            std_z(b)
            copy_score(b - 1, ps_m)
            normalise_z(b)
            gain_z(b)
            relu_h1(b, ps_q)
            relu_h2(b, ps_m)
            copy_score(b, ps_m)

        @block.vector
        def _(dve):
            def quad_form(s, k):
                dve.wait_ge(q_psum, s + 1)
                wait(dve, var_ready, s)
                n = GATHERS[k]
                nc.vector.tensor_tensor(quad[:, 0:n, :], ps_q[:, 0:n * D].rearrange("r (g d) -> r g d", d=D),
                                        emb[k][:, :, :], ALU.mult).then_inc(quad_ready, 1)

            def sum_quad(s, k):
                wait(dve, std_ready, s)
                dve.wait_ge(quad_ready, s + 1)
                n = GATHERS[k]
                nc.vector.tensor_reduce(var[:, 0:n], quad[:, 0:n, :], AX.X, ALU.add).then_inc(var_ready, 1)

            def scale_emb(s, b, k, par):
                n = GATHERS[k]
                dve.wait_ge(std_ready, s + 1)
                if k == 1:
                    dve.wait_ge(special_ready, b + 1)
                nc.vector.reciprocal(rstd[:, 0:n], std[:, 0:n]).then_inc(rstd_ready, 1)
                wait(dve, mix_psum, s - 1)
                dve.wait_ge(rstd_ready, s + 1)
                nc.vector.tensor_tensor(emb_r[par][:, :, :], emb[k][:, 0:REG, :],
                                        rstd[:, 0:REG].unsqueeze(2).to_broadcast([ROWS, REG, D]),
                                        ALU.mult).then_inc(emb_r_ready, 1)

            def scale_special(b):
                dve.wait_ge(rstd_ready, 4 * b + 1)
                wait(dve, mix_psum, 4 * b)
                nc.vector.tensor_tensor(emb_s[:, :, :], emb[0][:, REG:GA, :],
                                        rstd[:, REG:GA].unsqueeze(2).to_broadcast([ROWS, GA - REG, D]),
                                        ALU.mult).then_inc(special_ready, 1)

            def bias_y(s, h):
                if h == 0:
                    wait(dve, v_ready, s)
                dve.wait_ge(y_psum, 2 * s + 1 + h)
                n = SPS // 2
                src = ps_y[:, h * 512:(h + 1) * 512].rearrange("e (s p) -> e s p", p=P)
                nc.vector.tensor_tensor(y[:, h * n:(h + 1) * n, :], src,
                                        y_bias[:, :].unsqueeze(1).to_broadcast([E, n, P]),
                                        ALU.add).then_inc(y_ready, 1)

            def sum_squares(s):
                dve.wait_ge(ysq_ready, 2 * s + 2)
                nc.vector.tensor_reduce(yvar[:, :], ysq[:, :, :], AX.X, ALU.add).then_inc(yvar_ready, 1)

            def normalise_y(s, b, k, par):
                wait(dve, gram_psum, s - 1)
                dve.wait_ge(x_ready, b + 1)
                xk = x[:, :].rearrange("e (j k g) -> e k g j", j=SQ, k=STEPS)[:, k]
                nc.vector.tensor_copy(v[par][:, :, P].rearrange("e (g j) -> e g j", j=SQ), xk)
                dve.wait_ge(ystd_ready, s + 1)
                nc.vector.reciprocal(yrstd[:, :], ystd[:, :]).then_inc(yrstd_ready, 1)
                dve.wait_ge(yrstd_ready, s + 1)
                nc.vector.tensor_tensor(v[par][:, :, 0:P], y[:, :, :],
                                        yrstd[:, :].unsqueeze(2).to_broadcast([E, SPS, P]),
                                        ALU.mult).then_inc(v_ready, 1)

            def scale_x(b):
                dve.wait_ge(xstd_ready, b + 1)
                nc.vector.reciprocal(xrstd[:, :], xstd[:, :]).then_inc(xrstd_ready, 1)
                dve.wait_ge(xrstd_ready, b + 1)
                wait(dve, xt_psum, b)
                nc.vector.tensor_scalar(x_scaled[:, :], ps_x, xrstd[:, 0:1], None,
                                        ALU.mult).then_inc(x_scaled_ready, 1)

            def finish_x(b):
                dve.wait_ge(x_next_ready, b + 1)
                wait(dve, sumx_psum, b)
                nc.vector.tensor_copy(x[:, :], x_next[:, :]).then_inc(x_ready, 1)

            def copy_sumx(b):
                dve.wait_ge(sumx_psum, b + 1)
                wait(dve, zk_psum, b)
                nc.vector.tensor_copy(zc[:, SIDE_END - 2:SIDE_END - 1], ps_sum).then_inc(sumx_ready, 1)

            def transpose_gram(b):
                dve.wait_ge(gram_ready, 4 * b + 4)
                wait(dve, zc_ready, b)
                nc.vector.transpose(zt[:, :], gram[:, 0:P, :].rearrange("p q g -> p (q g)")).then_inc(zt_ready, 1)
                wait(dve, zk_psum, b)
                nc.vector.transpose(zc[:, SIDE_AT:SIDE_AT + 2 * P],
                                    gram[:, P:TC, :].rearrange("p q g -> p (q g)"))
                dve.wait_ge(zt_ready, b + 1)
                for packed, piece in pair_pieces(zt, zc):
                    last = nc.vector.tensor_copy(packed, piece)
                last.then_inc(zc_ready, 1)

            def stats_z(b):
                dve.wait_ge(z_psum, b + 1)
                nc.vector.bn_stats(stats[:, :], ps_a[:, :]).then_inc(stats_ready, 1)
                dve.wait_ge(stats_ready, b + 1)
                dve.nop(nofuse=True)
                nc.vector.bn_aggr(mv[:, :], stats[:, :]).then_inc(mv_ready, 1)

            def shift_z(b):
                dve.wait_ge(zstd_ready, b + 1)
                wait(dve, z_ready, b)
                nc.vector.reciprocal(zrstd[:, :], zstd[:, :]).then_inc(zrstd_ready, 1)
                dve.wait_ge(zrstd_ready, b + 1)
                nc.vector.tensor_scalar(zshift[:, :], zrstd[:, :], mv[:, 0:1], -1.0, ALU.mult,
                                        ALU.mult).then_inc(zshift_ready, 1)

            done = [0]

            def link(instruction):
                done[0] += 1
                instruction.then_inc(prep_dve, 1)
                dve.wait_ge(prep_dve, done[0])

            def fold_norm_over_p():
                dve.wait_ge(fold_in, FOLD_LOADS * DMA)
                a = coef[:, :, :]
                nc.vector.tensor_tensor(a[:, 0], bq[:, :], gp[:, :], ALU.mult)
                nc.vector.tensor_tensor(a[:, 1], bp[:, :], gq[:, :], ALU.mult)
                nc.vector.tensor_tensor(a[:, 2], gp[:, :], gq[:, :], ALU.mult)
                link(nc.vector.tensor_tensor(a[:, 3], bp[:, :], bq[:, :], ALU.mult))
                link(nc.vector.tensor_tensor(fold_q[:, :, :], isq[:, :, :],
                                             a[:, 1].unsqueeze(2).to_broadcast([128, KT, P]), ALU.mult))
                link(nc.vector.tensor_tensor(fold[:, :, P:2 * P], isp[:, :, :],
                                             a[:, 0].unsqueeze(2).to_broadcast([128, KT, P]), ALU.mult))
                link(nc.vector.tensor_tensor(fold[:, :, P:2 * P], fold[:, :, P:2 * P], fold_q[:, :, :], ALU.add))
                nc.vector.tensor_scalar(fold[:, :, SIDE - 1], a[:, 3], float(E), None, ALU.mult)
                nc.vector.tensor_copy(fold[0:P, KT - 1, SIDE - 2:SIDE - 1], bp[0:P, KT - 1:KT])
                link(nc.vector.tensor_scalar(fold[0:P, KT - 1, 0:P], ident[0:P, 0:P], gp[0:P, KT - 1:KT], None, ALU.mult))
                assert done[0] == DVE_FOLD

            nc.vector.memset(gram_w[:, :], 0.0)
            nc.vector.memset(ones[:, :], 1.0)
            nc.vector.memset(eps[:, :], EPS)
            nc.vector.memset(zc[:, SIDE_AT - 1:SIDE_AT], 0.0)
            nc.vector.memset(zc[:, SIDE_END - 1:SIDE_END], 1.0)
            nc.vector.memset(v[0][:, :, P + 1], 1.0)
            nc.vector.memset(v[1][:, :, P + 1], 1.0)
            link(nc.vector.memset(fold[:, :, :], 0.0))
            assert done[0] == DVE_CONST
            dve.wait_ge(ws_in, 4 * DMA)
            link(nc.vector.tensor_reduce(wc_mean[:, :], wc[:, :], AX.X, ALU.add))
            link(nc.vector.tensor_scalar(wc_mean[:, :], wc_mean[:, :], 1.0 / E, None, ALU.mult))
            link(nc.vector.tensor_scalar(wc[:, :], wc[:, :], wc_mean[:, 0:1], None, ALU.subtract))
            assert done[0] == DVE_WC
            link(nc.vector.tensor_tensor(wcg[:, :], wc[:, :], gs_b[:, :], ALU.mult))
            dve.wait_ge(prep_pe, PE_GRAM)
            nc.vector.tensor_copy(gram_w[0:D, 0:D], ps_a[0:D, 0:D])
            link(nc.vector.tensor_copy(gram_w[D:2 * D, D:2 * D], ps_a[D:2 * D, D:2 * D]))
            assert done[0] == DVE_GRAM
            dve.wait_ge(interaction_w_in, 2 * DMA)
            link(nc.vector.tensor_reduce(proj_mean[:, :], proj[:, :, :], AX.X, ALU.add))
            link(nc.vector.tensor_scalar(proj_mean[:, :], proj_mean[:, :], 1.0 / P, None, ALU.mult))
            link(nc.vector.tensor_tensor(proj[:, :, :], proj[:, :, :],
                                         proj_mean[:, :].unsqueeze(2).to_broadcast([ROWS, NPROJ, P]), ALU.subtract))
            assert done[0] == DVE_PROJ
            dve.wait_ge(x_w_in, 3 * DMA)
            link(nc.vector.tensor_reduce(wd_mean[:, :], wd[:, :, :], AX.X, ALU.add))
            link(nc.vector.scalar_tensor_tensor(
                wd[:, :, :], wd_mean[:, :].unsqueeze(2).to_broadcast([128, DK, E]), -1.0 / E, wd[:, :, :],
                ALU.mult, ALU.add))
            assert done[0] == DVE_WD
            fold_norm_over_p()
            quad_form(0, 0)
            sum_quad(0, 0)
            scale_emb(0, 0, 0, 0)
            scale_special(0)
            scale_x(0)
            quad_form(1, 1)
            sum_quad(1, 1)
            dve.wait_ge(prep_pe, PE_YBIAS)
            link(nc.vector.tensor_copy(y_bias[:, :], ps_y[:, 0:P]))
            assert done[0] == DVE_YBIAS
            finish_x(0)
            scale_emb(1, 0, 1, 1)
            quad_form(2, 2)

            def body(b, first, last):
                b2 = not isinstance(b, int) or b >= 2
                for k in range(STEPS):
                    i = 4 * b + k
                    bias_y(i, 0)
                    bias_y(i, 1)
                    if not (last and k >= 2):
                        sum_quad(i + 2, (k + 2) % STEPS)
                    if k == 2:
                        copy_sumx(b)
                    sum_squares(i)
                    if not (last and k >= 2):
                        scale_emb(i + 2, b + (k + 2) // STEPS, (k + 2) % STEPS, k % 2)
                    if k == 2 and not last:
                        scale_special(b + 1)
                    if k == 2 and not first:
                        stats_z(b - 1)
                    normalise_y(i, b, k, k % 2)
                    if k == 0 and not last:
                        scale_x(b + 1)
                    if k == 2 and not first:
                        shift_z(b - 1)
                    if k == 3 and not last:
                        finish_x(b + 1)
                    if not (last and k >= 1):
                        quad_form(i + 3, (k + 3) % STEPS)
                    if k == 0 and not first:
                        transpose_gram(b - 1)

            blocks(dve, body)
            transpose_gram(NBLK - 1)
            stats_z(NBLK - 1)
            shift_z(NBLK - 1)

        @block.tensor
        def _(pe):
            mm = nc.tensor.matmul

            def transpose_emb(s, b, k):
                pe.wait_ge(gathered[k], GATHERS[k] * DMA * (b + 1))
                wait(pe, emb_t_ready, s)
                for t in range(GATHERS[k] // 2):
                    last = nc.tensor.transpose(ps_t[:, t * ROWS:(t + 1) * ROWS],
                                               emb[k][:, 2 * t:2 * t + 2, :].rearrange("r g d -> r (g d)"),
                                               ident[:, :])
                last.then_inc(emb_t_psum, 1)

            def apply_gram_w(s, k, par):
                pe.wait_ge(emb_t_ready, s + 1)
                wait(pe, quad_ready, s)
                for t in range(GATHERS[k] // 2):
                    last = mm(ps_q[:, t * 128:(t + 1) * 128], emb_t[par][:, t * ROWS:(t + 1) * ROWS], gram_w[:, :],
                              start=True, stop=True)
                last.then_inc(q_psum, 1)

            def project(s, b, k, par):
                pe.wait_ge(emb_r_ready, s + 1)
                pe.wait_ge(special_ready, b + 1)
                wait(pe, mix_ready, s)
                width = (FULL + 1) * P
                for u in range(UNITS):
                    mm(ps_m[:, P + u * width:P + (u + 1) * width],
                       emb_r[par][:, 2 * u:2 * u + 2, :].rearrange("r g d -> r (g d)"),
                       proj[:, 0:FULL + 1, :].rearrange("r j p -> r (j p)"), start=(u == 0), stop=False,
                       skip_group_check=True)
                first = FULL + 1 + k * (1 + UNITS)
                fifths = ps_m[:, :].rearrange("m (c p) -> m c p", p=P)[:, 0:COLS:FULL + 1, :]
                mm(fifths, emb_s[:, :, :].rearrange("r g d -> r (g d)"),
                   proj[:, first:first + 1 + UNITS, :].rearrange("r j p -> r (j p)"), start=False, stop=True,
                   skip_group_check=True).then_inc(mix_psum, 1)

            def expand(s, par):
                pe.wait_ge(mix_ready, s + 1)
                for h in range(2):
                    wait(pe, y_ready, 2 * s - 1 + h)
                    mm(ps_y[:, h * 512:(h + 1) * 512], wcg[h * D:(h + 1) * D, :], mix[par][h * D:(h + 1) * D, :],
                       start=True, stop=True).then_inc(y_psum, 1)

            def gram_v(s, par):
                pe.wait_ge(v_ready, s + 1)
                wait(pe, gram_ready, s)
                for g in range(SPS // SQ):
                    for j in range(SQ):
                        m = SQ * g + j
                        last = mm(ps_z[32 * j:32 * j + 32, g * TC:(g + 1) * TC], v[par][:, m, 0:P],
                                  v[par][:, m, :], start=True, stop=True)
                last.then_inc(gram_psum, 1)

            def project_x(b):
                pe.wait_ge(dense_x_in, DMA * (b + 1))
                wait(pe, x_scaled_ready, b)
                wait(pe, z_t_ready, b - 2)
                for kt in range(DK):
                    last = mm(ps_x, dense_x[:, kt, :], wd[:, kt, :], start=(kt == 0), stop=(kt == DK - 1))
                last.then_inc(x_psum, 1)

            def transpose_x(b):
                pe.wait_ge(x_scaled_ready, b + 1)
                nc.tensor.transpose(ps_xt, x_scaled[:, :], ident[:, :]).then_inc(xt_psum, 1)

            def sum_x(b):
                pe.wait_ge(x_ready, b + 1)
                mm(ps_sum, x[:, :], ones[:, :], start=True, stop=True).then_inc(sumx_psum, 1)

            def transpose_z_pairs(b, x_blocks):
                pe.wait_ge(zc_ready, b + 1)
                pe.wait_ge(x_next_ready, x_blocks)
                if isinstance(b, int) and b == 0:
                    pe.wait_ge(prep_act, ACT_FOLD)
                elif isinstance(b, int) and b == NBLK - 1:
                    pe.wait_ge(h1_ready, b)
                else:
                    pe.wait_ge(score_ready, b)
                for t in range(KT - 1):
                    nc.tensor.transpose(ps_a[:, t * BLK:(t + 1) * BLK], zc[:, t * 128:(t + 1) * 128], ident[:, :])
                nc.tensor.transpose(ps_b[0:KL, 0:BLK], zc[:, 128 * (KT - 1):ZROWS], ident[:, :]).then_inc(zk_psum, 1)

            def z_first(b):
                pe.wait_ge(zk_ready, b + 1)
                for t in range(3):
                    mm(ps_a[:, :], zk[:, t, :], wl[:, t, :], start=(t == 0), stop=False)

            def z_second(b):
                for t in range(3, KT):
                    rows = 128 if t < KT - 1 else KL
                    last = mm(ps_a[:, :], zk[0:rows, t, :], wl[0:rows, t, :], start=False, stop=(t == KT - 1))
                last.then_inc(z_psum, 1)

            def transpose_z(b, x_blocks):
                pe.wait_ge(z_ready, b + 1)
                pe.wait_ge(sumx_ready, x_blocks)
                for t in range(ZK):
                    last = nc.tensor.transpose(ps_b[:, t * BLK:(t + 1) * BLK], z[:, t * 128:(t + 1) * 128], ident[:, :])
                last.then_inc(z_t_psum, 1)

            def top1(b):
                pe.wait_ge(dense_h_in, DMA * (b + 1))
                if isinstance(b, int) and b == 0:
                    pe.wait_ge(mlp_w_in, MLP_LOADS * DMA)
                for m in range(H1 // 128):
                    for kt in (*range(ZK, ZK + DK), *range(ZK)):
                        if m == 0 and kt == 0:
                            pe.wait_ge(z_t_ready, b + 1)
                        rhs = z_t[:, kt, :] if kt < ZK else dense_h[:, kt - ZK, :]
                        last = mm(ps_a[:, m * BLK:(m + 1) * BLK], w1_s[:, kt, m * 128:(m + 1) * 128], rhs,
                                  start=(kt == ZK), stop=(kt == ZK - 1))
                last.then_inc(h1_psum, 1)

            def top1_dense(b, ps):
                pe.wait_ge(dense_h_in, DMA * (b + 1))
                for kt in range(DK):
                    for m in range(H1 // 128):
                        mm(ps[:, m * BLK:(m + 1) * BLK], w1_s[:, ZK + kt, m * 128:(m + 1) * 128], dense_h[:, kt, :],
                           start=(kt == 0 and m == 0), stop=False, skip_group_check=True)

            def top1_z(b, ps):
                pe.wait_ge(z_t_ready, b + 1)
                for kt in range(ZK):
                    for m in range(H1 // 128):
                        last = mm(ps[:, m * BLK:(m + 1) * BLK], w1_s[:, kt, m * 128:(m + 1) * 128], z_t[:, kt, :],
                                  start=False, stop=(kt == ZK - 1), skip_group_check=True)
                last.then_inc(h1_psum, 1)

            def top2(b, ps):
                pe.wait_ge(h1_ready, b + 1)
                n = H1 // 128
                for m in range(H2 // 128):
                    for kt in range(n):
                        last = mm(ps[:, m * BLK:(m + 1) * BLK], w2_s[:, kt, m * 128:(m + 1) * 128], h1[:, kt, :],
                                  start=(kt == 0), stop=(kt == n - 1))
                last.then_inc(h2_psum, 1)

            def top3(b, ps):
                pe.wait_ge(h2_ready, b + 1)
                n = H2 // 128
                for kt in range(n):
                    last = mm(ps[:, H2:H2 + 1], h2[:, kt, :], w3_s[:, kt:kt + 1], start=(kt == 0), stop=(kt == n - 1))
                last.then_inc(score_psum, 1)

            def fold_wl(first_tile, end):
                pe.wait_ge(prep_dve, DVE_FOLD)
                pe.wait_ge(wl_in, KT * DMA)
                for t in range(first_tile, end):
                    last = mm(ps_a[0:SIDE, :], fold[:, t, :], wl[:, t, :], start=(t == 0), stop=(t == KT - 1))
                if end == KT:
                    last.then_inc(prep_pe, 1)

            pe.wait_ge(prep_dve, DVE_WC)
            nc.tensor.transpose(ps_a[:, 0:2 * D], wc[:, :], ident[:, :]).then_inc(prep_pe, 1)
            pe.wait_ge(prep_act, ACT_WCE)
            mm(ps_a[:, 0:2 * D], wc_e[:, :], wc_e[:, :], start=True, stop=True).then_inc(prep_pe, 1)
            pe.wait_ge(prep_dve, DVE_PROJ)
            mm(ps_y[:, 0:P], bs_b[:, :], proj[0:NF, 0, :], start=True, stop=True).then_inc(prep_pe, 1)
            transpose_emb(0, 0, 0)
            pe.wait_ge(prep_dve, DVE_WD)
            project_x(0)
            apply_gram_w(0, 0, 0)
            transpose_emb(1, 0, 1)
            apply_gram_w(1, 1, 1)
            transpose_x(0)
            project(0, 0, 0, 0)
            fold_wl(0, 3)
            transpose_emb(2, 0, 2)
            fold_wl(3, KT)
            apply_gram_w(2, 2, 0)
            pe.wait_ge(prep_dve, DVE_YBIAS)

            def first_block():
                for i in range(STEPS):
                    expand(i, i % 2)
                    if i == 0:
                        project_x(1)
                    if i == 1:
                        transpose_x(1)
                    project(i + 1, (i + 1) // STEPS, (i + 1) % STEPS, (i + 1) % 2)
                    if i > 0:
                        gram_v(i - 1, (i + 1) % 2)
                    if i == 1:
                        pe.wait_ge(x_next_ready, 2)
                        sum_x(0)
                    transpose_emb(i + 3, (i + 3) // STEPS, (i + 3) % STEPS)
                    apply_gram_w(i + 3, (i + 3) % STEPS, (i + 1) % 2)

            def body(b, first, last):
                if first:
                    first_block()
                    return
                b2 = not isinstance(b, int) or b >= 2
                for k in range(STEPS):
                    i = 4 * b + k
                    newest_last = not b2 and k < 2
                    expand(i, k % 2)
                    if k == 0:
                        if b2:
                            top2(b - 2, ps_a)
                        if not last:
                            project_x(b + 1)
                    if k == 2:
                        z_second(b - 1)
                    if k == 1 and not last:
                        transpose_x(b + 1)
                    if not (last and k >= 1) and not newest_last:
                        transpose_emb(i + 3, b + (k + 3) // STEPS, (k + 3) % STEPS)
                    if not (last and k == 3):
                        project(i + 1, b + (k + 1) // STEPS, (k + 1) % STEPS, (k + 1) % 2)
                    if k == 0 and b2:
                        top3(b - 2, ps_a)
                    if k == 1:
                        transpose_z_pairs(b - 1, NBLK if last else b + 2)
                    if k == 3:
                        transpose_z(b - 1, b + 1)
                    gram_v(i - 1, (k + 1) % 2)
                    if newest_last:
                        transpose_emb(i + 3, b + (k + 3) // STEPS, (k + 3) % STEPS)
                    if not (last and k >= 1):
                        apply_gram_w(i + 3, (k + 3) % STEPS, (k + 1) % 2)
                    if k == 1:
                        z_first(b - 1)
                        sum_x(b)
                    if k == 3:
                        top1(b - 1)

            blocks(pe, body)
            b = NBLK - 1
            gram_v(NS - 1, (NS - 1) % 2)
            top2(b - 1, ps_m)
            transpose_z_pairs(b, NBLK)
            z_first(b)
            z_second(b)
            top3(b - 1, ps_m)
            top1_dense(b, ps_q)
            transpose_z(b, NBLK)
            top1_z(b, ps_q)
            pe.wait_ge(score_ready, b)
            top2(b, ps_m)
            top3(b, ps_m)


def kernel(**inputs):
    import numpy as np
    import concourse.bacc as bacc
    from concourse.bass_utils import run_bass_kernel_spmd

    def f(name):
        return np.asarray(inputs[name])

    tables = [f(f"tbl_{n}") for n in range(NF)]
    base = np.cumsum([0] + [t.shape[0] for t in tables[:-1]]).astype(np.int32)
    wl = f("L0_rec_Wl")
    gsi, bsi = f("L0_rec_gsi"), f("L0_rec_bsi")
    wl_pairs = np.zeros((128, KT, MAXD), wl.dtype)
    of_p = np.zeros((128, KT), np.int64)
    of_q = np.zeros((128, KT), np.int64)
    is_p = np.zeros((128, KT, P), np.float32)
    is_q = np.zeros((128, KT, P), np.float32)
    b_of_p, b_of_q = np.zeros((2, 128, KT), bsi.dtype)
    rows_of_wl = set()
    for row, q, p in pair_order():
        r, t = row % 128, row // 128
        of_p[r, t], of_q[r, t] = p, q
        b_of_p[r, t], b_of_q[r, t] = bsi[p], bsi[q]
        is_p[r, t, p] = is_q[r, t, q] = 1.0
        if p > q and (q, p) not in rows_of_wl:
            rows_of_wl.add((q, p))
            wl_pairs[r, t] = wl[:, (p + 1) * p // 2 + q + 1]
    assert len(rows_of_wl) == P * (P - 1) // 2
    for p in range(P):
        of_p[p, KT - 1] = p
        b_of_p[p, KT - 1] = bsi[p]
        wl_pairs[p, KT - 1] = wl[:, (p + 1) * p // 2]

    def columns(a):
        return np.ascontiguousarray(a.reshape(-1, 128).T)

    def k_tiles(a):
        return np.ascontiguousarray(a.reshape(-1, 128, a.shape[1]).transpose(1, 0, 2))

    def in_order(a):
        shaped = a.reshape(*a.shape[:-1], NBLK, STEPS, SPS // SQ, SQ)
        return np.ascontiguousarray(np.moveaxis(shaped, -1, -3).reshape(a.shape))

    sample = np.zeros((ROWS, BGA), np.int64)
    feature = np.zeros((ROWS, BGA), np.int64)
    wsi_t = f("L0_rec_Wsi").T
    proj = np.zeros((ROWS, FULL + 1 + STEPS * (1 + UNITS), P), wsi_t.dtype)
    for k in range(STEPS):
        for h in range(2):
            first = SPS * k + COLS * h
            for u in range(UNITS):
                g = sum(GATHERS[:k]) + 2 * u + h
                sample[:, g] = first + 1 + (FULL + 1) * u + np.arange(ROWS) // NF
                feature[:, g] = np.arange(ROWS) % NF
                rest = FULL * NF + REST * (UNITS * k + u) + np.arange(REST)
                sample[rest, REG + h] = first + (FULL + 1) * (u + 1)
                feature[rest, REG + h] = HEAD + np.arange(REST)
                proj[rest, FULL + 1 + k * (1 + UNITS) + 1 + u] = wsi_t[HEAD:]
            own = slice(k * NF, (k + 1) * NF)
            sample[own, REG + h] = first
            feature[own, REG + h] = np.arange(NF)
            proj[own, FULL + 1 + k * (1 + UNITS)] = wsi_t
    for j in range(FULL):
        proj[j * NF:(j + 1) * NF, j] = wsi_t
    proj[FULL * NF:, FULL] = wsi_t[:HEAD]
    ids = f("ids").reshape(NBLK, BLK, NF)[:, sample, feature]

    w1 = f("W_top1")
    arrays = {
        "dense_t": k_tiles(in_order(f("r_dense_t").T)),
        "ids": np.ascontiguousarray(ids.transpose(1, 0, 2).reshape(ROWS, -1)),
        "row_base": base[feature[:, 0:GA]],
        "tables": np.concatenate(tables, axis=0),
        "ws_t": np.ascontiguousarray(f("L0_rec_Ws").T),
        "gs": f("L0_rec_gs"),
        "bs": f("L0_rec_bs"),
        "wsi_t": proj,
        "wd_t": k_tiles(f("L0_rec_Wd").T),
        "gd": columns(f("L0_rec_gd")),
        "bd": columns(f("L0_rec_bd")),
        "wl_pairs": wl_pairs,
        "g_of_p": gsi[of_p],
        "g_of_q": gsi[of_q],
        "b_of_p": b_of_p,
        "b_of_q": b_of_q,
        "is_p": is_p,
        "is_q": is_q,
        "identity": np.eye(128, dtype=np.float32),
        "gl": columns(f("L0_rec_gl")[:DIMS]),
        "bl": columns(f("L0_rec_bl")[:DIMS]),
        "w1": k_tiles(np.concatenate([w1[:DIMS], w1[MAXD:]], axis=0)),
        "b1": columns(f("b_top1")),
        "w2": k_tiles(f("W_top2")),
        "b2": columns(f("b_top2")),
        "w3": columns(f("W_top3").reshape(-1)),
    }
    nc = bacc.Bacc("TRN2", target_bir_lowering=False, num_devices=1)
    args = [nc.dram_tensor(f"in_{name}", a.shape, mybir.dt.from_np(a.dtype), kind="ExternalInput").ap()
            for name, a in arrays.items()]
    out = nc.dram_tensor("scores", (BLK, NBLK), F32, kind="ExternalOutput").ap()
    dlrm_kernel(nc, *args, out)
    r = run_bass_kernel_spmd(nc, [{f"in_{name}": a for name, a in arrays.items()}], core_ids=[0])
    return np.moveaxis(r.results[0]["scores"].T.reshape(NBLK, SQ, STEPS, SPS // SQ), 1, -1).reshape(B, 1)
```
